# Optimizing a Trainium2 kernel written in Bass

```python
import numpy as np
import jax
import jax.numpy as jnp

def _softmax(x, axis=-1):
    return jax.nn.softmax(x, axis=axis)

def _gelu(x):
    return jax.nn.gelu(x, approximate=True)

def _silu(x):
    return jax.nn.silu(x)

def _sigmoid(x):
    return jax.nn.sigmoid(x)

def _layernorm(x, axis=-1, eps=1e-05):
    m = jnp.mean(x, axis=axis, keepdims=True)
    v = jnp.var(x, axis=axis, keepdims=True)
    return (x - m) / jnp.sqrt(v + eps)

def _scatter_add(tgt, idx, src, axis=0):
    return tgt.at[idx].add(src)

def _segment_sum(src, seg, n):
    return jax.ops.segment_sum(src, seg, n)
kernel_name = 'mk_prb_d1_jaxref_r4_e43d69'

def setup_inputs(seed: int=0):
    np.random.seed(seed)
    _w = jnp.asarray

    def _L0_attn_setup():
        import jax, jax.numpy as jnp
        import numpy as np
        import math
        D_MODEL = 256
        NUM_HEADS = 16
        D_HEAD = D_MODEL // NUM_HEADS
        N_FREQ = D_HEAD // 2 + 1
        COMPRESSION_RATIO = 0.5

        def _spectral_filter(t, mask):
            tf = jnp.fft.rfft(t, axis=-1)
            tf = tf * mask
            return jnp.fft.irfft(tf, n=t.shape[-1], axis=-1).astype(t.dtype)
        key = jax.random.key(seed)
        k_x, k_qkv, k_out, k_b, k_m = jax.random.split(key, 5)
        B, S = (2, 512)
        x = jax.random.normal(k_x, (B, S, D_MODEL), dtype=jnp.float32)
        w_qkv = jax.random.normal(k_qkv, (D_MODEL, 3 * D_MODEL), dtype=jnp.float32) / math.sqrt(D_MODEL)
        w_out = jax.random.normal(k_out, (D_MODEL, D_MODEL), dtype=jnp.float32) / math.sqrt(D_MODEL)
        b_out = jax.random.normal(k_b, (D_MODEL,), dtype=jnp.float32) * 0.01
        init_logit = math.log(COMPRESSION_RATIO / (1.0 - COMPRESSION_RATIO))
        mask_logits = init_logit + 0.1 * jax.random.normal(k_m, (N_FREQ,), dtype=jnp.float32)
        return {'x': x, 'w_qkv': w_qkv, 'w_out': w_out, 'b_out': b_out, 'mask_logits': mask_logits}
    _L0_attn_in = _L0_attn_setup()

    def _L0_ffn_setup():
        import jax, jax.numpy as jnp
        import numpy as np
        import math
        BETA = 0.9
        THRESHOLD = 1.0
        NUM_STEPS = 5
        ALPHA = 2.0

        @jax.custom_vjp
        def spike_fn(u):
            return (u > 0).astype(u.dtype)

        def _spike_fwd(u):
            return (spike_fn(u), u)

        def _spike_bwd(u, g):
            s = jnp.pi / 2.0 * ALPHA * u
            return (g * (ALPHA / 2.0) / (1.0 + s * s),)
        spike_fn.defvjp(_spike_fwd, _spike_bwd)
        key = jax.random.key(seed)
        k1, k2, k3 = jax.random.split(key, 3)
        n_embd = 256
        x = jax.random.normal(k1, (4, 512, n_embd), dtype=jnp.float32)
        W_fc = jax.random.normal(k2, (4 * n_embd, n_embd), dtype=jnp.float32) / math.sqrt(n_embd)
        W_proj = jax.random.normal(k3, (n_embd, 4 * n_embd), dtype=jnp.float32) / math.sqrt(4 * n_embd)
        return {'x': x, 'W_fc': W_fc, 'W_proj': W_proj}
    _L0_ffn_in = _L0_ffn_setup()
    _d = {'L0_attn_x': _L0_attn_in['x'], 'L0_attn_w_qkv': _L0_attn_in['w_qkv'], 'L0_attn_w_out': _L0_attn_in['w_out'], 'L0_attn_b_out': _L0_attn_in['b_out'], 'L0_attn_mask_logits': _L0_attn_in['mask_logits'], 'L0_ffn_W_fc': _L0_ffn_in['W_fc'], 'L0_ffn_W_proj': _L0_ffn_in['W_proj']}
    _x0 = _d['L0_attn_x']
    _d['L0_attn_x'] = jax.random.normal(jax.random.fold_in(jax.random.key(seed), 1), (2, 2048, 256), dtype=_x0.dtype)
    del _x0
    return _d

def reference(L0_attn_x, L0_attn_w_qkv, L0_attn_w_out, L0_attn_b_out, L0_attn_mask_logits, L0_ffn_W_fc, L0_ffn_W_proj):

    def _L0_attn_ref(x, w_qkv, w_out, b_out, mask_logits):
        import jax, jax.numpy as jnp
        import numpy as np
        import math
        D_MODEL = 256
        NUM_HEADS = 16
        D_HEAD = D_MODEL // NUM_HEADS
        N_FREQ = D_HEAD // 2 + 1
        COMPRESSION_RATIO = 0.5

        def _spectral_filter(t, mask):
            tf = jnp.fft.rfft(t, axis=-1)
            tf = tf * mask
            return jnp.fft.irfft(tf, n=t.shape[-1], axis=-1).astype(t.dtype)
        B, S, D = x.shape
        H, dh = (NUM_HEADS, D_HEAD)
        qkv = x @ w_qkv
        q, k, v = jnp.split(qkv, 3, axis=-1)
        to_heads = lambda t: t.reshape(B, S, H, dh).transpose(0, 2, 1, 3)
        q, k, v = (to_heads(q), to_heads(k), to_heads(v))
        mask = jax.nn.sigmoid(mask_logits)
        q = _spectral_filter(q, mask)
        k = _spectral_filter(k, mask)
        scores = jnp.einsum('bhqd,bhkd->bhqk', q, k) / math.sqrt(dh)
        attn = jax.nn.softmax(scores, axis=-1)
        out = jnp.einsum('bhqk,bhkd->bhqd', attn, v)
        out = out.transpose(0, 2, 1, 3).reshape(B, S, D)
        return out @ w_out + b_out

    def _L0_ffn_ref(x, W_fc, W_proj):
        import jax, jax.numpy as jnp
        import numpy as np
        import math
        BETA = 0.9
        THRESHOLD = 1.0
        NUM_STEPS = 5
        ALPHA = 2.0

        @jax.custom_vjp
        def spike_fn(u):
            return (u > 0).astype(u.dtype)

        def _spike_fwd(u):
            return (spike_fn(u), u)

        def _spike_bwd(u, g):
            s = jnp.pi / 2.0 * ALPHA * u
            return (g * (ALPHA / 2.0) / (1.0 + s * s),)
        spike_fn.defvjp(_spike_fwd, _spike_bwd)
        h = jnp.square(jax.nn.relu(jnp.einsum('bsd,fd->bsf', x, W_fc)))
        y = jnp.einsum('bsf,df->bsd', h, W_proj)

        def step(mem, _):
            reset = jax.lax.stop_gradient(spike_fn(mem - THRESHOLD))
            mem_new = BETA * mem + y - reset * THRESHOLD
            spk = spike_fn(mem_new - THRESHOLD)
            return (mem_new, spk)
        mem0 = jnp.zeros_like(y)
        _, spks = jax.lax.scan(step, mem0, None, length=NUM_STEPS)
        return jnp.sum(spks, axis=0) / NUM_STEPS
    x = L0_attn_x
    xn = _layernorm(x, axis=-1)
    x = x + _L0_attn_ref(xn, L0_attn_w_qkv, L0_attn_w_out, L0_attn_b_out, L0_attn_mask_logits) + _L0_ffn_ref(xn, L0_ffn_W_fc, L0_ffn_W_proj)
    return x

_drawn_inputs = setup_inputs


def setup_inputs(seed=0):
    import zlib

    import numpy as np

    out = dict(_drawn_inputs(seed))
    spreads = {}
    factors = {'L0_attn_b_out': 7.009, 'L0_attn_mask_logits': 35.705}
    for name, (base, spread) in spreads.items():
        noise = np.random.default_rng([zlib.crc32(name.encode()), seed]).standard_normal(out[name].shape)
        drawn = base * np.exp(spread * noise) if base else spread * noise
        out[name] = jnp.asarray(drawn.astype(out[name].dtype))
    for name, factor in factors.items():
        out[name] = (out[name] * factor).astype(out[name].dtype)
    return out
```

```python
from contextlib import ExitStack

import numpy as np

import concourse.bass as bass
from concourse import mybir


P = 128
B, S, D = 2, 2048, 256
H, DH = 16, 16
F = 4 * D
NF = DH // 2 + 1
TOK = B * S
KC = D // P
NT = TOK // P
TB = S // P
BLK = 512
NB = TOK // BLK
KT = BLK // P
QB = 2 * H * DH // P
FC = F // P
HALF = S // 2
ROWS = 4 * DH + 2
UNITS = 2 * TB
STEPS = 2 * TB
LEAD = 8
LAG = 2
FIRST = 6
PS = 4
USES = 7
STACK = 7 * 16
SPIKES = 5
BETA = 0.9
EPS = 1e-5
SCALE = float(DH) ** -0.5

F32 = mybir.dt.float32
F32R = mybir.dt.float32r
BF16 = mybir.dt.bfloat16
ALU = mybir.AluOpType
ACT = mybir.ActivationFunctionType
AX = mybir.AxisListType.X


def build(nc, x, wqk, wv, wout, bout, logits, wfc, wproj, basis, eye, out):
    with ExitStack() as ctx:
        def sb(name, shape, dt=F32):
            return ctx.enter_context(nc.sbuf_tensor(name, shape, dt))

        def sem(name):
            return ctx.enter_context(nc.semaphore(name))

        qk_dram = nc.dram_tensor("qk_scratch", [2, H, 2, DH, TOK], F32, kind="Internal").ap()
        zero_dram = nc.dram_tensor("zero_scratch", [2, S], F32, kind="Internal").ap()

        xnT = sb("xnT", [P, KC, TOK])
        v_all = sb("v_all", [P, NT, D])
        attn = sb("attn", [P, NT, D])
        counts = sb("counts", [P, NT, D], BF16)
        qst = [sb(f"qst{i}", [ROWS, S], F32R) for i in range(2)]
        kst = [sb(f"kst{i}", [ROWS, S], F32R) for i in range(2)]
        probs = sb("probs", [P, PS, HALF])
        vst = [sb(f"vst{i}", [P, TB, 32]) for i in range(2)]
        wfc_sb = sb("wfc_sb", [P, KC, F])
        wproj_sb = sb("wproj_sb", [P, FC, D])
        wout_sb = sb("wout_sb", [P, KC, D])
        bout_sb = sb("bout_sb", [P, D])
        ident = sb("ident", [P, P])
        relu_sb = sb("relu_sb", [P, FC, P])
        hid_sb = sb("hid_sb", [P, FC, P])
        y_sb = sb("y_sb", [P, D])
        lif = sb("lif", [P, 7, D])
        oT = sb("oT", [P, 2, D])
        pmax = sb("pmax", [P, TB, 4])
        nmax = sb("nmax", [P, 8])
        shift = sb("shift", [P, 16])
        shiftT = sb("shiftT", [16, P])
        rden = sb("rden", [P, 2, 4])
        stats = sb("stats", [P, KT, 6])
        meanvar = sb("meanvar", [P, KT, 2])
        rstd = sb("rstd", [P, 5, KT])
        carrier = sb("carrier", [P, 2])
        filt = sb("filt", [P, 3, NF])

        x_in = attn[:, 0:2 * KT, :].rearrange("p (b k) d -> p b k d", b=2)
        x_norm = attn[:, 2 * KT:4 * KT, :].rearrange("p (b k) d -> p b k d", b=2)
        xb = probs[:, 0:2, :].rearrange("p b (c t) -> p b c t", c=KC)
        hilo = probs[:, 2:4, :].rearrange("p b (c t) -> p b c t", c=2)
        early = counts[:, :, :].bitcast(F32).rearrange("p a b -> p (a b)")
        basis_sb = early[:, 0:NF * P].rearrange("p (f e) -> p f e", f=NF)
        at = NF * P
        wqk_raw = early[:, at:at + QB * D].rearrange("p (b d) -> p b d", b=QB)
        at += QB * D
        wqk_sb = early[:, at:at + KC * QB * P].rearrange("p (c e) -> p c e", c=KC)
        at += KC * QB * P
        wv_sb = early[:, at:at + KC * D].rearrange("p (c e) -> p c e", c=KC)
        at += KC * D
        filter_sb = early[:, at:at + P]
        assert at + 2 * P <= NT * D // 2
        filter_acc = [filter_sb, early[:, at + P:at + 2 * P]]
        x_end = probs[:, 0:2, :].rearrange("p b (k d) -> p b k d", k=KT)
        sum_end = probs[:, 2:4, :].rearrange("p b (k d) -> p b k d", k=KT)
        attn_end = v_all[:, 0:2 * KT, :].rearrange("p (b k) d -> p b k d", b=2)
        attnT_end = v_all[:, 2 * KT:4 * KT, :].rearrange("p (b k) d -> p b (k d)", b=2)
        out_end = v_all[:, 4 * KT:6 * KT, :].rearrange("p (b k) d -> p b k d", b=2)

        st = ctx.enter_context(nc.psum_tensor("st", [P, 2, HALF], F32))
        mx = ctx.enter_context(nc.psum_tensor("mx", [P, 2, BLK], F32))
        po = ctx.enter_context(nc.psum_tensor("po", [P, BLK], F32))
        misc = ctx.enter_context(nc.psum_tensor("misc", [P, BLK], F32))

        const_in = sem("const_in")
        late_in = sem("late_in")
        preset = sem("preset")
        zero_out = sem("zero_out")
        filt_act = sem("filt_act")
        filt_dve = sem("filt_dve")
        fold_done = sem("fold_done")
        fold_taken = sem("fold_taken")
        x_landed = [sem(f"x_landed{i}") for i in range(2)]
        ln_step = sem("ln_step")
        var_ready = sem("var_ready")
        std_ready = sem("std_ready")
        ln_done = sem("ln_done")
        tr_done = sem("tr_done")
        xb_ready = sem("xb_ready")
        xnt_copied = sem("xnt_copied")
        qk_ready = sem("qk_ready")
        hi_ready = sem("hi_ready")
        lo_done = sem("lo_done")
        stored = [sem(f"stored{i}") for i in range(2)]
        v_ready = sem("v_ready")
        v_taken = sem("v_taken")
        stack_in = [sem(f"stack_in{i}") for i in range(2)]
        mx_ready = sem("mx_ready")
        mx_taken = sem("mx_taken")
        max_step = sem("max_step")
        shift_split = sem("shift_split")
        shift_in = sem("shift_in")
        score_ready = sem("score_ready")
        exp_done = sem("exp_done")
        pv_done = sem("pv_done")
        vst_ready = sem("vst_ready")
        po_taken = sem("po_taken")
        misc_full = sem("misc_full")
        misc_taken = sem("misc_taken")
        den_ready = sem("den_ready")
        squared = sem("squared")
        lif_step = sem("lif_step")
        lif_done = sem("lif_done")
        end_x = [sem(f"end_x{i}") for i in range(2)]
        end_staged = sem("end_staged")
        end_bias = sem("end_bias")
        end_tr = sem("end_tr")
        end_trT = sem("end_trT")
        end_proj = sem("end_proj")
        end_base = sem("end_base")
        end_sum = sem("end_sum")
        end_out = [sem(f"end_out{i}") for i in range(2)]

        x_blocks = x.rearrange("b (n k p) d -> (b n) p k d", k=KT, p=P)
        out_blocks = out.rearrange("b (n k p) d -> (b n) p k d", k=KT, p=P)

        def use(i, k):
            return USES * i + 1 + k

        UP_A, SHIFT_1, UP_B, DOWN, OUT_0, SHIFT_0, OUT_1 = range(USES)

        def out_1(last):
            return OUT_1 - 1 if last else OUT_1

        def qk_psum(w):
            return (mx[:, 0, :], mx[:, 1, :], po[:, :], misc[:, :])[w]

        block = ctx.enter_context(nc.Block())

        @block.sync
        def _(sp):
            def load_x(t, p):
                sp.dma_start(x_in[:, p], x_blocks[t]).then_inc(x_landed[p], 16)

            load_x(0, 0)
            sp.dma_start(ident[:], eye).then_inc(const_in, 16)
            sp.dma_start(filt[:, 0, :], logits.partition_broadcast(P)).then_inc(const_in, 16)
            sp.dma_start(basis_sb, basis).then_inc(const_in, 16)
            sp.dma_start(wqk_raw, wqk).then_inc(const_in, 16)
            sp.dma_start(wv_sb, wv.rearrange("(c p) e -> p c e", p=P)).then_inc(const_in, 16)
            load_x(1, 1)
            sp.dma_start(wfc_sb[:], wfc.rearrange("(c p) e -> p c e", p=P)).then_inc(late_in, 16)
            sp.dma_start(wproj_sb[:], wproj.rearrange("(c p) e -> p c e", p=P)).then_inc(late_in, 16)
            sp.dma_start(wout_sb[:], wout.rearrange("(c p) e -> p c e", p=P)).then_inc(late_in, 16)
            sp.dma_start(bout_sb[:], bout.partition_broadcast(P)).then_inc(late_in, 16)
            sp.wait_ge(preset, 1)
            for r in range(2):
                for c in range(2):
                    sp.dma_start(zero_dram[r:r + 1, c * HALF:(c + 1) * HALF],
                                 probs[0:1, 3, :]).then_inc(zero_out, 16)

            def store_block(t, p):
                for w in range(QB):
                    g, s = w % 2, w % 2
                    sp.wait_ge(lo_done, QB * t + w + 1 + QB)
                    for part in range(2):
                        dst = qk_dram[w // 2, g * 8:(g + 1) * 8, part, :, bass.ds(t * BLK, BLK)]
                        sp.dma_start(dst, hilo[:, s, part, :]).then_inc(stored[s], 16)

            with sp.Fori(0, NB // 2 - 1) as n:
                for p in range(2):
                    t = 2 * n + p
                    sp.wait_ge(ln_done, t + 1)
                    load_x(t + 2, p)
                    store_block(t, p)
            for t in range(NB - 2, NB):
                store_block(t, t % 2)

            def load_stack(h, b):
                tok = slice(b * S, (b + 1) * S)
                for part in range(2):
                    for dup in range(2):
                        r = (2 * part + dup) * DH
                        sp.dma_start(qst[b][r:r + DH, :].bitcast(F32), qk_dram[0, h, part, :, tok]).then_inc(stack_in[b], 16)
                sp.dma_start(qst[b][4 * DH:ROWS, :].bitcast(F32), zero_dram).then_inc(stack_in[b], 16)
                for dup in range(2):
                    r = dup * 2 * DH
                    src = qk_dram[1, h, :, :, tok].rearrange("r d t -> (r d) t")
                    sp.dma_start(kst[b][r:r + 2 * DH, :].bitcast(F32), src).then_inc(stack_in[b], 16)

            def store_shift(n, b, half):
                sp.wait_ge(misc_taken, n[1] + 1)
                for r in range(2):
                    dst = qst[b][4 * DH + r:4 * DH + r + 1, half * HALF:(half + 1) * HALF]
                    sp.dma_start(dst.bitcast(F32), shiftT[8 * r:8 * r + 8, :]).then_inc(shift_in, 16)

            for s in range(2):
                sp.wait_ge(stored[s], 32 * (QB * NB // 2 + 1))
            sp.wait_ge(zero_out, 64)
            load_stack(0, 0)
            store_shift((0, 0), 0, 0)

            def head(h, b, last=False):
                i = 2 * h + b
                if not last:
                    sp.wait_ge(exp_done, STEPS * i + 2)
                    load_stack(h + b, 1 - b)
                store_shift((None, use(i, SHIFT_1)), b, 1)
                if not last:
                    store_shift((None, use(i, SHIFT_0)), 1 - b, 0)

            with sp.Fori(0, H - 1) as h:
                for b in range(B):
                    head(h, b)
            head(H - 1, 0)
            head(H - 1, 1, last=True)

            def end_load(t, p):
                sp.dma_start(x_end[:, p], x_blocks[t]).then_inc(end_x[p], 16)

            sp.wait_ge(pv_done, STEPS * NT + PS)
            end_load(0, 0)
            end_load(1, 1)

            def end_store(t, p):
                sp.wait_ge(end_sum, t + 2)
                sp.dma_start(out_blocks[t], out_end[:, p]).then_inc(end_out[p], 16)

            with sp.Fori(0, NB // 2 - 1) as n:
                for p in range(2):
                    t = 2 * n + p
                    sp.wait_ge(end_bias, t + 1)
                    end_load(t + 2, p)
                    end_store(t, p)
            for t in range(NB - 2, NB):
                end_store(t, t % 2)
            for p in range(2):
                sp.wait_ge(end_out[p], 16 * (NB // 2 + 1))

        @block.gpsimd
        def _(pool):
            pool.memset(probs[0:1, 3, :], 0.0).then_inc(preset, 1)
            pool.wait_ge(preset, 1)
            pool.memset(lif[:, 4, :], 0.0).then_inc(preset, 1)
            for i in range(2):
                pool.wait_ge(preset, 2 + 3 * i)
                pool.memset(kst[i][4 * DH:ROWS, :].bitcast(F32), 1.0).then_inc(preset, 1)
                pool.wait_ge(preset, 3 + 3 * i)
                pool.memset(vst[i][:, :, DH:DH + 1], 1.0).then_inc(preset, 1)
                pool.wait_ge(preset, 4 + 3 * i)
                pool.memset(vst[i][:, :, DH + 1:32], 0.0).then_inc(preset, 1)
            pool.sem_inc(tr_done, 2)
            pool.sem_inc(xnt_copied, 2)
            pool.sem_inc(lo_done, QB)
            pool.sem_inc(mx_taken, 2)
            pool.sem_inc(exp_done, 2)
            pool.sem_inc(pv_done, PS)
            for s in range(2):
                pool.sem_inc(stored[s], 32)
                pool.sem_inc(end_out[s], 16)
            pool.sem_inc(squared, 2)
            for free in (v_taken, lif_done, end_tr, end_trT, end_proj, end_sum):
                pool.sem_inc(free, 1)

            with pool.Fori(0, NB // 2) as n:
                for p in range(2):
                    t = 2 * n + p
                    pool.wait_ge(xb_ready, t + 1)
                    pool.tensor_copy(xnT[:, :, bass.ds(t * BLK, BLK)], xb[:, p]).then_inc(xnt_copied, 1)

            def stage_v(h, b, after):
                pool.wait_ge(pv_done, after)
                pool.tensor_copy(vst[b][:, :, 0:DH],
                                 v_all[:, b * TB:(b + 1) * TB, bass.ds(h * DH, DH)]).then_inc(vst_ready, 1)

            pool.wait_ge(v_taken, NB + 1)
            stage_v(0, 0, PS)

            mem, decayed, upd, acc, zeros, *spks = (lif[:, k, :] for k in range(7))
            LIF_LINKS = 4 * (SPIKES - 1) + 2

            def head(h, b, last=False):
                i = 2 * h + b
                if not last:
                    stage_v(h + b, 1 - b, STEPS * i + PS)
                for part, k in enumerate((UP_A, UP_B)):
                    c = slice(part * FC // 2, (part + 1) * FC // 2)
                    pool.wait_ge(misc_taken, use(i, k) + 1)
                    pool.tensor_tensor(hid_sb[:, c], relu_sb[:, c], relu_sb[:, c], ALU.mult).then_inc(squared, 1)
                n = LIF_LINKS * i
                pool.wait_ge(misc_taken, use(i, DOWN) + 1)
                pool.tensor_tensor(acc, zeros, zeros, ALU.add)
                pool.tensor_scalar(spks[0], y_sb[:], 1.0, None, ALU.is_gt)
                pool.tensor_scalar(decayed, y_sb[:], BETA, None, ALU.mult).then_inc(lif_step, 1)
                for step in range(1, SPIKES):
                    pool.wait_ge(lif_step, n + 1)
                    pool.tensor_tensor(upd, decayed, y_sb[:], ALU.add).then_inc(lif_step, 1)
                    pool.wait_ge(lif_step, n + 2)
                    pool.tensor_tensor(mem, upd, spks[(step + 1) % 2], ALU.subtract).then_inc(lif_step, 1)
                    pool.wait_ge(lif_step, n + 3)
                    pool.tensor_tensor(acc, acc, spks[(step + 1) % 2], ALU.add).then_inc(lif_step, 1)
                    pool.tensor_scalar(spks[step % 2], mem, 1.0, None, ALU.is_gt)
                    pool.tensor_scalar(decayed, mem, BETA, None, ALU.mult).then_inc(lif_step, 1)
                    n += 4
                pool.wait_ge(lif_step, n + 1)
                pool.tensor_tensor(acc, acc, spks[(SPIKES - 1) % 2], ALU.add).then_inc(lif_step, 1)
                pool.wait_ge(lif_step, n + 2)
                pool.tensor_tensor(carrier[:, 1:2], zeros[:, 0:1], zeros[:, 0:1], ALU.add)
                pool.tensor_copy(counts[:, bass.ds(i, 1), :].rearrange("p a d -> p (a d)"), acc).then_inc(lif_done, 1)

            with pool.Fori(0, H - 1) as h:
                for b in range(B):
                    head(h, b)
            head(H - 1, 0)
            head(H - 1, 1, last=True)

            pool.wait_ge(pv_done, STEPS * NT + PS)
            with pool.Fori(0, NB // 2) as n:
                for p in range(2):
                    t = 2 * n + p
                    if p == 0:
                        pool.wait_ge(misc_taken, use(NT - 1, out_1(True)) + 1)
                    pool.wait_ge(end_tr, t + 1)
                    pool.tensor_copy(attn_end[:, p], attn[:, bass.ds(t * KT, KT), :]).then_inc(end_staged, 1)
                    pool.wait_ge(end_x[p], 16 * (n + 1))
                    pool.wait_ge(end_sum, t + 1)
                    pool.wait_ge(late_in, 64)
                    pool.tensor_tensor(sum_end[:, p], x_end[:, p],
                                       bout_sb[:, :].rearrange("p (k d) -> p k d", k=1).broadcast_to([P, KT, D]),
                                       ALU.add).then_inc(end_bias, 1)

        @block.scalar
        def _(act):
            act.wait_ge(const_in, 80)
            act.activation(filt[:, 1, :], filt[:, 0, :], ACT.Exp, scale=-1.0).then_inc(filt_act, 1)
            act.wait_ge(fold_done, 1)
            act.activation(wqk_sb, st[:, 0, :].rearrange("p (c e) -> p c e", c=KC), ACT.Copy).then_inc(fold_taken, 1)

            def deviation(t):
                act.wait_ge(var_ready, t + 1)
                act.activation(rstd[:, 1, :], rstd[:, 0, :], ACT.Sqrt).then_inc(std_ready, 1)

            def take_transposed(t, p):
                act.wait_ge(tr_done, t + 1 + 2)
                act.wait_ge(xnt_copied, t + 1)
                act.activation(xb[:, p], st[:, 0, :].rearrange("p (c e) -> p c e", c=KC),
                               ACT.Copy).then_inc(xb_ready, 1)

            def take_products(t, n, p):
                for w in range(QB):
                    s = w % 2
                    act.wait_ge(qk_ready, QB * t + w + 1)
                    act.wait_ge(stored[s], 32 * ((QB // 2) * t + w // 2 + 1))
                    act.activation(hilo[:, s, 0, :].bitcast(F32R), qk_psum(w), ACT.Copy).then_inc(hi_ready, 1)
                act.wait_ge(v_ready, t + 1)
                act.activation(v_all[:, bass.ds(t * KT, KT), :], st[:, 1, :].rearrange("p (k d) -> p k d", k=KT),
                               ACT.Copy).then_inc(v_taken, 1)

            act.wait_ge(preset, 1)
            act.wait_ge(zero_out, 64)
            deviation(0)
            take_transposed(0, 0)
            with act.Fori(0, NB // 2 - 1) as n:
                for p in range(2):
                    t = 2 * n + p
                    deviation(t + 1)
                    take_transposed(t + 1, 1 - p)
                    take_products(t, n, p)
            deviation(NB - 1)
            take_transposed(NB - 1, 1)
            take_products(NB - 2, NB // 2 - 1, 0)
            take_products(NB - 1, NB // 2 - 1, 1)

            def take_shift(u, landed):
                act.wait_ge(misc_full, u + 1)
                act.wait_ge(shift_in, 32 * landed)
                act.activation(shiftT[:, :].bitcast(F32R), misc[0:16, 0:P], ACT.Copy).then_inc(misc_taken, 1)

            def exponentials(g, s):
                act.wait_ge(score_ready, g + 1)
                act.wait_ge(pv_done, g + 1)
                act.activation(probs[:, s % PS, :], st[:, s % 2, :], ACT.Exp, scale=SCALE).then_inc(exp_done, 1)

            def take_output(i, half):
                act.wait_ge(pv_done, STEPS * i + (half + 1) * TB + PS)
                act.activation(oT[:, half, :], po[:, half * D:(half + 1) * D], ACT.Copy).then_inc(po_taken, 1)

            def head(h, b, last=False):
                i = 2 * h + b
                for s in range(FIRST, STEPS + FIRST):
                    if s < STEPS or not last:
                        exponentials(STEPS * i + s, s)
                    if s in (8, 14):
                        k, part = (UP_A, 0) if s == 8 else (UP_B, 1)
                        act.wait_ge(misc_full, use(i, k) + 1)
                        act.wait_ge(squared, 2 * i + part + 1)
                        act.activation(relu_sb[:, part * FC // 2:(part + 1) * FC // 2, :],
                                       misc[:, :].rearrange("p (f t) -> p f t", f=FC // 2),
                                       ACT.Relu).then_inc(misc_taken, 1)
                    if s == 11:
                        take_shift(use(i, SHIFT_1), 2 * i + 1)
                    if s == 18:
                        take_output(i, 0)
                    if s == 20:
                        act.wait_ge(misc_full, use(i, DOWN) + 1)
                        act.wait_ge(lif_done, i + 1)
                        act.activation(y_sb[:], misc[:, 0:D], ACT.Copy).then_inc(misc_taken, 1)
                    if s == 27 and not last:
                        take_shift(use(i, SHIFT_0), 2 * i + 2)
                    if s == 34:
                        take_output(i, 1)

            take_shift(0, 0)
            act.wait_ge(xnt_copied, NB + 2)
            for s in range(2):
                act.wait_ge(stored[s], 32 * (QB * NB // 2 + 1))
            for s in range(FIRST):
                exponentials(s, s)
            with act.Fori(0, H - 1) as h:
                for b in range(B):
                    head(h, b)
            head(H - 1, 0)
            head(H - 1, 1, last=True)

            with act.Fori(0, NB // 2) as n:
                for p in range(2):
                    t = 2 * n + p
                    act.wait_ge(end_tr, t + 2)
                    act.wait_ge(end_proj, t + 1)
                    act.activation(attnT_end[:, p], st[:, 0, :], ACT.Copy).then_inc(end_trT, 1)

        @block.tensor
        def _(pe):
            pe.wait_ge(const_in, 80)
            pe.wait_ge(filt_dve, NF + 2)
            for w in range(QB):
                for c in range(KC):
                    mm = pe.matmul(st[:, 0, c * BLK + w * P:c * BLK + (w + 1) * P],
                                   wqk_raw[:, w, c * P:(c + 1) * P], filter_acc[(NF - 1) % 2], start=True, stop=True)
            mm.then_inc(fold_done, 1)
            pe.wait_ge(fold_taken, 1)

            def transpose_block(t, p):
                pe.wait_ge(ln_done, t + 1)
                pe.wait_ge(xb_ready, t)
                for c in range(KC):
                    for k in range(KT):
                        mm = pe.transpose(st[:, 0, c * BLK + k * P:c * BLK + (k + 1) * P],
                                          x_norm[:, p, k, c * P:(c + 1) * P], ident[:])
                mm.then_inc(tr_done, 1)

            def project_block(t, p):
                pe.wait_ge(xb_ready, t + 1)
                for w in range(QB):
                    pe.wait_ge(lo_done, QB * t + w + 1)
                    for c in range(KC):
                        mm = pe.matmul(qk_psum(w), wqk_sb[:, c, w * P:(w + 1) * P], xb[:, p, c, :],
                                       start=(c == 0), stop=(c == KC - 1))
                    mm.then_inc(qk_ready, 1)
                pe.wait_ge(v_taken, t + 1)
                for k in range(KT):
                    for c in range(KC):
                        mm = pe.matmul(st[:, 1, k * D:(k + 1) * D], xb[:, p, c, k * P:(k + 1) * P], wv_sb[:, c, :],
                                       start=(c == 0), stop=(c == KC - 1))
                mm.then_inc(v_ready, 1)

            transpose_block(0, 0)
            with pe.Fori(0, NB // 2 - 1) as n:
                for p in range(2):
                    t = 2 * n + p
                    transpose_block(t + 1, 1 - p)
                    project_block(t, p)
            transpose_block(NB - 1, 1)
            project_block(NB - 2, 0)
            project_block(NB - 1, 1)

            def max_chunk(n, unit, b, c):
                tile, chunk = unit // 2, 2 * (unit % 2) + c
                pe.wait_ge(mx_taken, n + 1)
                pe.matmul(mx[:, c, :], qst[b][:, tile * P:(tile + 1) * P], kst[b][:, chunk * BLK:(chunk + 1) * BLK],
                          start=True, stop=True).then_inc(mx_ready, 1)

            def transpose_shift(n, u):
                pe.wait_ge(shift_split, n + 1)
                pe.wait_ge(misc_taken, u)
                pe.matmul(misc[0:16, 0:P], shift[:], ident[:], start=True, stop=True).then_inc(misc_full, 1)

            def scores(g, s, b):
                half, kt = s // TB, s % TB
                pe.wait_ge(exp_done, g + 1)
                for c in range(2):
                    q = half * HALF + c * BLK
                    mm = pe.matmul(st[:, s % 2, c * BLK:(c + 1) * BLK], kst[b][:, kt * P:(kt + 1) * P],
                                   qst[b][:, q:q + BLK], start=True, stop=True)
                mm.then_inc(score_ready, 1)

            def times_v(g, s, b):
                half, kt = s // TB, s % TB
                pe.wait_ge(exp_done, g + 1 + 2)
                for j in range(4):
                    mm = pe.matmul(po[32 * j:32 * (j + 1), half * D:(half + 1) * D], vst[b][:, kt, :],
                                   probs[:, s % PS, j * D:(j + 1) * D], start=(kt == 0), stop=(kt == TB - 1))
                mm.then_inc(pv_done, 1)

            def slot(h, b, s, last=False):
                i = 2 * h + b
                g = STEPS * i + s
                if s < STEPS or not last:
                    if s % STEPS == 0:
                        pe.wait_ge(shift_in, 32 * (2 * i + (3 if s else 1)))
                    if s == TB:
                        pe.wait_ge(shift_in, 32 * (2 * i + 2))
                    scores(g, s % STEPS, b if s < STEPS else 1 - b)
                unit = (s - LEAD) % UNITS
                maxima = s < LEAD or not last
                mb = b if s < LEAD else 1 - b
                if s == LEAD and maxima:
                    pe.wait_ge(stack_in[mb], STACK * (h + 1 + b))
                n = 2 * (g + UNITS - LEAD)
                if maxima:
                    max_chunk(n, unit, mb, 0)
                if s >= LAG and (s - LAG < STEPS or not last):
                    v = s - LAG
                    if v % TB == 0:
                        e = 2 * i + v // TB
                        pe.wait_ge(po_taken, e)
                        pe.wait_ge(vst_ready, i + 1 + v // STEPS)
                    times_v(g - LAG, v % STEPS, b if v < STEPS else 1 - b)
                if maxima:
                    max_chunk(n + 1, unit, mb, 1)

            def up(i, f0, k, tok, last_of):
                for f in (f0, f0 + 1):
                    for c in range(KC):
                        mm = pe.matmul(misc[:, (f % 4) * P:(f % 4 + 1) * P], wfc_sb[:, c, f * P:(f + 1) * P],
                                       xnT[:, c, bass.ds(tok, P)], start=(c == 0), stop=(c == KC - 1))
                if last_of:
                    mm.then_inc(misc_full, 1)

            def down(f0, last_of):
                for f in (f0, f0 + 1):
                    mm = pe.matmul(misc[:, 0:D], hid_sb[:, f, :], wproj_sb[:, f, :],
                                   start=(f == 0), stop=(f == FC - 1))
                if last_of:
                    mm.then_inc(misc_full, 1)

            def turn_output(i, half, u):
                pe.wait_ge(misc_taken, u)
                pe.wait_ge(po_taken, 2 * i + half + 1)
                for c in range(2):
                    mm = pe.transpose(misc[:, c * P:(c + 1) * P], oT[:, half, c * P:(c + 1) * P], ident[:])
                mm.then_inc(misc_full, 1)

            def head(h, b, last=False):
                i = 2 * h + b
                for s in range(FIRST, STEPS + FIRST):
                    slot(h, b, s, last)
                    if s == 6:
                        pe.wait_ge(misc_taken, use(i, UP_A))
                        up(i, 0, UP_A, i * P, False)
                    if s == 7:
                        up(i, 2, UP_A, i * P, True)
                    if s == 10:
                        transpose_shift(2 * i + 1, use(i, SHIFT_1))
                    if s == 12:
                        pe.wait_ge(misc_taken, use(i, UP_B))
                        up(i, 4, UP_B, i * P, False)
                    if s == 13:
                        up(i, 6, UP_B, i * P, True)
                    if 16 <= s < 20:
                        if s == 16:
                            pe.wait_ge(misc_taken, use(i, DOWN))
                            pe.wait_ge(squared, 2 * i + 2 + 2)
                        down(2 * (s - 16), s == 19)
                    if s == 21:
                        turn_output(i, 0, use(i, OUT_0))
                    if s == 26 and not last:
                        transpose_shift(2 * i + 2, use(i, SHIFT_0))
                    if s == 36:
                        turn_output(i, 1, use(i, out_1(last)))

            pe.wait_ge(stack_in[0], STACK)
            pe.wait_ge(preset, 8)
            pe.wait_ge(lo_done, QB * NB + QB)
            pe.wait_ge(v_taken, NB + 1)
            pe.wait_ge(late_in, 64)
            pe.wait_ge(xnt_copied, NB + 2)
            for unit in range(TB):
                for c in range(2):
                    max_chunk(2 * unit + c, unit, 0, c)
            for unit in range(TB, UNITS - LEAD):
                for c in range(2):
                    max_chunk(2 * unit + c, unit, 0, c)
                if unit == TB + 2:
                    pe.wait_ge(shift_split, 1)
                    pe.matmul(misc[0:16, 0:P], shift[:], ident[:], start=True, stop=True).then_inc(misc_full, 1)
            for s in range(FIRST):
                slot(0, 0, s)
            with pe.Fori(0, H - 1) as h:
                for b in range(B):
                    head(h, b)
            head(H - 1, 0)
            head(H - 1, 1, last=True)

            def end_transpose(t, p):
                pe.wait_ge(end_staged, t + 1)
                pe.wait_ge(end_trT, t + 1)
                for c in range(KC):
                    for k in range(KT):
                        mm = pe.transpose(st[:, 0, c * BLK + k * P:c * BLK + (k + 1) * P],
                                          attn_end[:, p, k, c * P:(c + 1) * P], ident[:])
                mm.then_inc(end_tr, 1)

            def end_project(t, p):
                pe.wait_ge(end_trT, t + 2)
                pe.wait_ge(end_sum, t + 1)
                for k in range(KT):
                    for c in range(KC):
                        mm = pe.matmul(st[:, 1, k * D:(k + 1) * D],
                                       attnT_end[:, p, c * BLK + k * P:c * BLK + (k + 1) * P], wout_sb[:, c, :],
                                       start=(c == 0), stop=(c == KC - 1))
                mm.then_inc(end_proj, 1)

            with pe.Fori(0, NB // 2) as n:
                for p in range(2):
                    t = 2 * n + p
                    end_transpose(t, p)
                    end_project(t, p)

        @block.vector
        def _(dve):
            dve.wait_ge(filt_act, 1)
            dve.tensor_scalar(filt[:, 2, :], filt[:, 1, :], 1.0, None, ALU.add).then_inc(filt_dve, 1)
            dve.wait_ge(filt_dve, 1)
            dve.reciprocal(filt[:, 0, :], filt[:, 2, :]).then_inc(filt_dve, 1)
            dve.wait_ge(filt_dve, 2)
            for f in range(NF):
                to, gate = filter_acc[f % 2], filt[:, 0, f:f + 1]
                if f == 0:
                    dve.tensor_scalar(to, basis_sb[:, f, :], gate, None, ALU.mult).then_inc(filt_dve, 1)
                else:
                    dve.wait_ge(filt_dve, f + 2)
                    dve.scalar_tensor_tensor(out=to, in0=basis_sb[:, f, :], scalar=gate, in1=filter_acc[1 - f % 2],
                                             op0=ALU.mult, op1=ALU.add).then_inc(filt_dve, 1)

            LN_LINKS = 7

            def normalise(t, n, p):
                base = LN_LINKS * t
                dve.wait_ge(x_landed[p], 16 * (n + 1))
                for k in range(KT):
                    last = dve.bn_stats(stats[:, k, :], x_in[:, p, k, :])
                last.then_inc(ln_step, 1)
                dve.wait_ge(ln_step, base + 1)
                dve.memset(carrier[:, 0:1], 0.0)
                for k in range(KT):
                    last = dve.bn_aggr(meanvar[:, k, :], stats[:, k, :])
                last.then_inc(ln_step, 1)
                dve.wait_ge(ln_step, base + 2)
                dve.tensor_scalar(rstd[:, 0, :], meanvar[:, :, 1], EPS, None, ALU.add).then_inc(var_ready, 1)
                dve.wait_ge(std_ready, t + 1)
                dve.reciprocal(rstd[:, 2, :], rstd[:, 1, :]).then_inc(ln_step, 1)
                dve.wait_ge(ln_step, base + 3)
                dve.tensor_tensor(rstd[:, 3, :], rstd[:, 2, :], rstd[:, 2, :], ALU.mult).then_inc(ln_step, 1)
                dve.wait_ge(ln_step, base + 4)
                dve.tensor_tensor(rstd[:, 4, :], rstd[:, 3, :], rstd[:, 0, :], ALU.mult).then_inc(ln_step, 1)
                dve.wait_ge(ln_step, base + 5)
                dve.tensor_scalar(rstd[:, 3, :], rstd[:, 4, :], -0.5, 1.5, ALU.mult, ALU.add).then_inc(ln_step, 1)
                dve.wait_ge(ln_step, base + 6)
                dve.tensor_tensor(rstd[:, 4, :], rstd[:, 3, :], rstd[:, 2, :], ALU.mult).then_inc(ln_step, 1)
                dve.wait_ge(ln_step, base + 7)
                dve.wait_ge(tr_done, t + 1)
                for k in range(KT):
                    last = dve.tensor_scalar(x_norm[:, p, k, :], x_in[:, p, k, :], meanvar[:, k, 0:1],
                                             rstd[:, 4, k:k + 1], ALU.subtract, ALU.mult)
                last.then_inc(ln_done, 1)

            def low_parts(t):
                for w in range(QB):
                    s = w % 2
                    dve.wait_ge(hi_ready, QB * t + w + 1)
                    dve.tensor_tensor(hilo[:, s, 1, :].bitcast(F32R), qk_psum(w), hilo[:, s, 0, :],
                                      ALU.subtract).then_inc(lo_done, 1)

            normalise(0, 0, 0)
            with dve.Fori(0, NB // 2 - 1) as n:
                for p in range(2):
                    t = 2 * n + p
                    normalise(t + 1, n + p, 1 - p)
                    low_parts(t)
            normalise(NB - 1, NB // 2 - 1, 1)
            low_parts(NB - 2)
            low_parts(NB - 1)

            def max_chunk(n, unit, c):
                dve.wait_ge(mx_ready, n + 1)
                tile, chunk = unit // 2, 2 * (unit % 2) + c
                dve.tensor_reduce(pmax[:, tile, chunk:chunk + 1], mx[:, c, :], AX, ALU.max).then_inc(mx_taken, 1)

            def split_shift(n, half, chunks):
                dve.wait_ge(mx_taken, chunks + 2)
                dve.tensor_reduce(nmax[:], pmax[:, half * 8:half * 8 + 8, :], AX, ALU.max, negate=True).then_inc(max_step, 1)
                dve.wait_ge(max_step, 2 * n + 1)
                dve.tensor_copy(shift[:, 0:8].bitcast(F32R), nmax[:]).then_inc(max_step, 1)
                dve.wait_ge(max_step, 2 * n + 2)
                dve.tensor_tensor(shift[:, 8:16].bitcast(F32R), nmax[:], shift[:, 0:8],
                                  ALU.subtract).then_inc(shift_split, 1)

            def normalise_output(h, b, half, u, n):
                dve.wait_ge(misc_full, u + 1)
                o = misc[:, 0:2 * P].rearrange("p (c j e) -> p c j e", c=2, j=4)
                dve.reciprocal(rden[:], o[:, :, :, DH]).then_inc(den_ready, 1)
                dve.wait_ge(den_ready, n + 1)
                tiles = attn[:, b * TB + half * 8:b * TB + half * 8 + 8, bass.ds(h * DH, DH)]
                dve.tensor_tensor(tiles.rearrange("p (j c) e -> p c j e", c=2), o[:, :, :, 0:DH],
                                  rden[:, :, :].rearrange("p c (j a) -> p c j a", a=1).broadcast_to([P, 2, 4, DH]),
                                  ALU.mult).then_inc(misc_taken, 1)

            for unit in range(TB):
                for c in range(2):
                    max_chunk(2 * unit + c, unit, c)
            split_shift(0, 0, 2 * TB)
            for unit in range(TB, UNITS - LEAD):
                for c in range(2):
                    max_chunk(2 * unit + c, unit, c)
            for s in range(FIRST):
                for c in range(2):
                    max_chunk(2 * (s + UNITS - LEAD) + c, (s - LEAD) % UNITS, c)

            def head(h, b, last=False):
                i = 2 * h + b
                for s in range(FIRST, STEPS + FIRST):
                    n = 2 * (STEPS * i + s + UNITS - LEAD)
                    if s < LEAD or not last:
                        for c in range(2):
                            max_chunk(n + c, (s - LEAD) % UNITS, c)
                    if s == LEAD - 1:
                        split_shift(2 * i + 1, 1, n + 2)
                    if s == 22:
                        normalise_output(h, b, 0, use(i, OUT_0), 2 * i)
                    if s == LEAD + TB - 1 and not last:
                        split_shift(2 * i + 2, 0, n + 2)
                    if s == STEPS + FIRST - 1:
                        normalise_output(h, b, 1, use(i, out_1(last)), 2 * i + 1)

            with dve.Fori(0, H - 1) as h:
                for b in range(B):
                    head(h, b)
            head(H - 1, 0)
            head(H - 1, 1, last=True)

            dve.wait_ge(lif_done, NT + 1)
            with dve.Fori(0, NB // 2) as n:
                for p in range(2):
                    t = 2 * n + p
                    dve.wait_ge(end_bias, t + 1)
                    dve.wait_ge(end_out[p], 16 * n + 16)
                    dve.scalar_tensor_tensor(out=out_end[:, p], in0=counts[:, bass.ds(t * KT, KT), :],
                                             scalar=1.0 / SPIKES, in1=sum_end[:, p],
                                             op0=ALU.mult, op1=ALU.add).then_inc(end_base, 1)
                    dve.wait_ge(end_base, t + 1)
                    dve.wait_ge(end_proj, t + 2)
                    dve.tensor_tensor(out_end[:, p], st[:, 1, :].rearrange("p (k d) -> p k d", k=KT),
                                      out_end[:, p], ALU.add).then_inc(end_sum, 1)


def filter_basis():
    e = np.arange(DH)
    one = np.zeros((NF, DH, DH))
    for f in range(NF):
        weight = 1.0 if f in (0, DH // 2) else 2.0
        one[f] = weight / DH * np.cos(2 * np.pi * f * (e[:, None] - e[None, :]) / DH)
    full = np.zeros((P, NF, P), np.float32)
    for g in range(P // DH):
        full[g * DH:(g + 1) * DH, :, g * DH:(g + 1) * DH] = one.transpose(1, 0, 2)
    return full


def kernel(L0_attn_x, L0_attn_w_qkv, L0_attn_w_out, L0_attn_b_out, L0_attn_mask_logits, L0_ffn_W_fc, L0_ffn_W_proj):
    import concourse.bacc as bacc
    from concourse.bass_utils import run_bass_kernel_spmd

    w_qkv = np.asarray(L0_attn_w_qkv)
    wqk = w_qkv[:, 0:2 * D].T.reshape(QB, P, D).transpose(1, 0, 2)
    arrays = {
        "x": np.asarray(L0_attn_x),
        "wqk": wqk,
        "wv": w_qkv[:, 2 * D:3 * D],
        "wout": np.asarray(L0_attn_w_out),
        "bout": np.asarray(L0_attn_b_out),
        "logits": np.asarray(L0_attn_mask_logits),
        "wfc": np.asarray(L0_ffn_W_fc).T,
        "wproj": np.asarray(L0_ffn_W_proj).T,
        "basis": filter_basis(),
        "eye": np.eye(P, dtype=np.float32),
    }
    arrays = {name: np.ascontiguousarray(a) for name, a in arrays.items()}
    nc = bacc.Bacc("TRN2", target_bir_lowering=False, num_devices=1)
    args = {
        name: nc.dram_tensor(name, a.shape, mybir.dt.from_np(a.dtype), kind="ExternalInput").ap()
        for name, a in arrays.items()
    }
    out = nc.dram_tensor("out", (B, S, D), F32, kind="ExternalOutput").ap()
    build(nc, out=out, **args)
    r = run_bass_kernel_spmd(nc, [arrays], core_ids=[0])
    return r.results[0]["out"]
```

```python
from contextlib import ExitStack

import numpy as np

import concourse.bass as bass
from concourse import mybir


P = 128
B, S, D = 2, 2048, 256
H, DH = 16, 16
F = 4 * D
NF = DH // 2 + 1
TOK = B * S
KC = D // P
NT = TOK // P
TB = S // P
BLK = 512
NB = TOK // BLK
KT = BLK // P
QB = 2 * H * DH // P
FC = F // P
HALF = S // 2
ROWS = 4 * DH + 2
UNITS = 2 * TB
STEPS = 2 * TB
LEAD = 8
LAG = 2
FIRST = 6
PS = 4
USES = 5
STACK = 7 * 16
SPIKES = 5
BETA = 0.9
EPS = 1e-5
SCALE = float(DH) ** -0.5

F32 = mybir.dt.float32
F32R = mybir.dt.float32r
BF16 = mybir.dt.bfloat16
ALU = mybir.AluOpType
ACT = mybir.ActivationFunctionType
AX = mybir.AxisListType.X


def build(nc, x, wqk, wv, wout, bout, logits, wfc, wproj, basis, eye, out):
    with ExitStack() as ctx:
        def sb(name, shape, dt=F32):
            return ctx.enter_context(nc.sbuf_tensor(name, shape, dt))

        def sem(name):
            return ctx.enter_context(nc.semaphore(name))

        qk_dram = nc.dram_tensor("qk_scratch", [2, H, 2, DH, TOK], F32, kind="Internal").ap()
        zero_dram = nc.dram_tensor("zero_scratch", [2, S], F32, kind="Internal").ap()

        xnT = sb("xnT", [P, KC, TOK])
        v_all = sb("v_all", [P, NT, D])
        attn = sb("attn", [P, NT, D])
        counts = sb("counts", [P, NT, D], BF16)
        qst = [sb(f"qst{i}", [ROWS, S], F32R) for i in range(2)]
        kst = [sb(f"kst{i}", [ROWS, S], F32R) for i in range(2)]
        probs = sb("probs", [P, PS, HALF])
        vst = [sb(f"vst{i}", [P, TB, 32]) for i in range(2)]
        wfc_sb = sb("wfc_sb", [P, KC, F])
        wproj_sb = sb("wproj_sb", [P, FC, D])
        wout_sb = sb("wout_sb", [P, KC, D])
        bout_sb = sb("bout_sb", [P, D])
        ident = sb("ident", [P, P])
        relu_sb = sb("relu_sb", [P, FC, P])
        hid_sb = sb("hid_sb", [P, FC, P])
        y_sb = sb("y_sb", [P, D])
        lif = sb("lif", [P, 7, D])
        o_sb = sb("o_sb", [P, 2, TB // 2, 32])
        pmax = sb("pmax", [P, TB, 4])
        nmax = sb("nmax", [P, 8])
        shift = sb("shift", [P, 16])
        shiftT = sb("shiftT", [16, P])
        rden = sb("rden", [P, TB // 2])
        stats = sb("stats", [P, KT, 6])
        meanvar = sb("meanvar", [P, KT, 2])
        rstd = sb("rstd", [P, 5, KT])
        carrier = sb("carrier", [P, 2])
        filt = sb("filt", [P, 3, NF])

        x_in = attn[:, 0:2 * KT, :].rearrange("p (b k) d -> p b k d", b=2)
        x_norm = attn[:, 2 * KT:4 * KT, :].rearrange("p (b k) d -> p b k d", b=2)
        xb = probs[:, 0:2, :].rearrange("p b (c t) -> p b c t", c=KC)
        hilo = probs[:, 2:4, :].rearrange("p b (c t) -> p b c t", c=2)
        early = counts[:, :, :].bitcast(F32).rearrange("p a b -> p (a b)")
        basis_sb = early[:, 0:NF * P].rearrange("p (f e) -> p f e", f=NF)
        at = NF * P
        wqk_raw = early[:, at:at + QB * D].rearrange("p (b d) -> p b d", b=QB)
        at += QB * D
        wqk_sb = early[:, at:at + KC * QB * P].rearrange("p (c e) -> p c e", c=KC)
        at += KC * QB * P
        wv_sb = early[:, at:at + KC * D].rearrange("p (c e) -> p c e", c=KC)
        at += KC * D
        filter_sb = early[:, at:at + P]
        assert at + 2 * P <= NT * D // 2
        filter_acc = [filter_sb, early[:, at + P:at + 2 * P]]
        x_end = [t[:, :, :].rearrange("p f t -> p (f t)").rearrange("p (k d) -> p k d", k=KT)
                 for t in (relu_sb, hid_sb)]
        attn_end = v_all[:, 0:2 * KT, :].rearrange("p (b k) d -> p b k d", b=2)
        attnT_end = v_all[:, 2 * KT:4 * KT, :].rearrange("p (b k) d -> p b (k d)", b=2)
        out_end = v_all[:, 4 * KT:6 * KT, :].rearrange("p (b k) d -> p b k d", b=2)

        st = ctx.enter_context(nc.psum_tensor("st", [P, 2, HALF], F32))
        banks = ctx.enter_context(nc.psum_tensor("banks", [P, 4, BLK], F32))
        mx, po, misc = banks[:, 0:2, :], banks[:, 2, :], banks[:, 3, :]
        proj_end = banks[:, :, :].rearrange("p (b k) (c d) -> p b (k c) d", b=2, c=2)

        const_in = sem("const_in")
        late_in = sem("late_in")
        preset = sem("preset")
        zero_out = sem("zero_out")
        filt_act = sem("filt_act")
        filt_dve = sem("filt_dve")
        fold_done = sem("fold_done")
        fold_taken = sem("fold_taken")
        x_landed = [sem(f"x_landed{i}") for i in range(2)]
        ln_step = sem("ln_step")
        var_ready = sem("var_ready")
        std_ready = sem("std_ready")
        ln_done = sem("ln_done")
        tr_done = sem("tr_done")
        xb_ready = sem("xb_ready")
        xnt_copied = sem("xnt_copied")
        qk_ready = sem("qk_ready")
        hi_ready = sem("hi_ready")
        lo_done = sem("lo_done")
        stored = [sem(f"stored{i}") for i in range(2)]
        v_ready = sem("v_ready")
        v_taken = sem("v_taken")
        stack_in = [sem(f"stack_in{i}") for i in range(2)]
        mx_ready = sem("mx_ready")
        mx_taken = sem("mx_taken")
        max_step = sem("max_step")
        shift_split = sem("shift_split")
        shift_in = sem("shift_in")
        score_ready = sem("score_ready")
        exp_done = sem("exp_done")
        pv_done = sem("pv_done")
        vst_ready = sem("vst_ready")
        po_taken = sem("po_taken")
        misc_full = sem("misc_full")
        misc_taken = sem("misc_taken")
        den_ready = sem("den_ready")
        normalised = sem("normalised")
        squared = sem("squared")
        lif_step = sem("lif_step")
        lif_done = sem("lif_done")
        end_x = [sem(f"end_x{i}") for i in range(2)]
        end_staged = sem("end_staged")
        end_bias = sem("end_bias")
        end_tr = sem("end_tr")
        end_trT = sem("end_trT")
        end_proj = sem("end_proj")
        end_base = sem("end_base")
        end_sum = sem("end_sum")
        end_out = [sem(f"end_out{i}") for i in range(2)]

        x_blocks = x.rearrange("b (n k p) d -> (b n) p k d", k=KT, p=P)
        out_blocks = out.rearrange("b (n k p) d -> (b n) p k d", k=KT, p=P)

        def use(i, k):
            return USES * i + 1 + k

        UP_A, SHIFT_1, UP_B, DOWN, SHIFT_0 = range(USES)

        def qk_psum(w):
            return banks[:, w, :]

        block = ctx.enter_context(nc.Block())

        @block.sync
        def _(sp):
            def load_x(t, p):
                sp.dma_start(x_in[:, p], x_blocks[t]).then_inc(x_landed[p], 16)

            load_x(0, 0)
            sp.dma_start(ident[:], eye).then_inc(const_in, 16)
            sp.dma_start(filt[:, 0, :], logits.partition_broadcast(P)).then_inc(const_in, 16)
            sp.dma_start(basis_sb, basis).then_inc(const_in, 16)
            sp.dma_start(wqk_raw, wqk).then_inc(const_in, 16)
            sp.dma_start(wv_sb, wv.rearrange("(c p) e -> p c e", p=P)).then_inc(const_in, 16)
            load_x(1, 1)
            sp.dma_start(wfc_sb[:], wfc.rearrange("(c p) e -> p c e", p=P)).then_inc(late_in, 16)
            sp.dma_start(wproj_sb[:], wproj.rearrange("(c p) e -> p c e", p=P)).then_inc(late_in, 16)
            sp.dma_start(wout_sb[:], wout.rearrange("(c p) e -> p c e", p=P)).then_inc(late_in, 16)
            sp.dma_start(bout_sb[:], bout.partition_broadcast(P)).then_inc(late_in, 16)
            sp.wait_ge(preset, 1)
            for r in range(2):
                for c in range(2):
                    sp.dma_start(zero_dram[r:r + 1, c * HALF:(c + 1) * HALF],
                                 probs[0:1, 3, :]).then_inc(zero_out, 16)

            def store_block(t, p):
                for w in range(QB):
                    g, s = w % 2, w % 2
                    sp.wait_ge(lo_done, QB * t + w + 1 + QB)
                    for part in range(2):
                        dst = qk_dram[w // 2, g * 8:(g + 1) * 8, part, :, bass.ds(t * BLK, BLK)]
                        sp.dma_start(dst, hilo[:, s, part, :]).then_inc(stored[s], 16)

            with sp.Fori(0, NB // 2 - 1) as n:
                for p in range(2):
                    t = 2 * n + p
                    sp.wait_ge(ln_done, t + 1)
                    load_x(t + 2, p)
                    store_block(t, p)
            for t in range(NB - 2, NB):
                store_block(t, t % 2)

            def load_stack(h, b):
                tok = slice(b * S, (b + 1) * S)
                for part in range(2):
                    for dup in range(2):
                        r = (2 * part + dup) * DH
                        sp.dma_start(qst[b][r:r + DH, :].bitcast(F32), qk_dram[0, h, part, :, tok]).then_inc(stack_in[b], 16)
                sp.dma_start(qst[b][4 * DH:ROWS, :].bitcast(F32), zero_dram).then_inc(stack_in[b], 16)
                for dup in range(2):
                    r = dup * 2 * DH
                    src = qk_dram[1, h, :, :, tok].rearrange("r d t -> (r d) t")
                    sp.dma_start(kst[b][r:r + 2 * DH, :].bitcast(F32), src).then_inc(stack_in[b], 16)

            def store_shift(n, b, half):
                sp.wait_ge(misc_taken, n[1] + 1)
                for r in range(2):
                    dst = qst[b][4 * DH + r:4 * DH + r + 1, half * HALF:(half + 1) * HALF]
                    sp.dma_start(dst.bitcast(F32), shiftT[8 * r:8 * r + 8, :]).then_inc(shift_in, 16)

            for s in range(2):
                sp.wait_ge(stored[s], 32 * (QB * NB // 2 + 1))
            sp.wait_ge(zero_out, 64)
            load_stack(0, 0)
            store_shift((0, 0), 0, 0)

            def head(h, b, last=False):
                i = 2 * h + b
                if not last:
                    sp.wait_ge(exp_done, STEPS * i + 2)
                    load_stack(h + b, 1 - b)
                store_shift((None, use(i, SHIFT_1)), b, 1)
                if not last:
                    store_shift((None, use(i, SHIFT_0)), 1 - b, 0)

            with sp.Fori(0, H - 1) as h:
                for b in range(B):
                    head(h, b)
            head(H - 1, 0)
            head(H - 1, 1, last=True)

            def end_load(t, p):
                sp.dma_start(x_end[p], x_blocks[t]).then_inc(end_x[p], 16)

            sp.wait_ge(misc_full, use(NT - 1, DOWN) + 1)
            end_load(0, 0)
            end_load(1, 1)

            def end_store(t, p):
                sp.wait_ge(end_sum, t + 3)
                sp.dma_start(out_blocks[t], out_end[:, p]).then_inc(end_out[p], 16)

            with sp.Fori(0, NB // 2 - 1) as n:
                for p in range(2):
                    t = 2 * n + p
                    sp.wait_ge(end_base, t + 1)
                    end_load(t + 2, p)
                    end_store(t, p)
            for t in range(NB - 2, NB):
                end_store(t, t % 2)
            for p in range(2):
                sp.wait_ge(end_out[p], 16 * (NB // 2 + 1))

        @block.gpsimd
        def _(pool):
            pool.memset(probs[0:1, 3, :], 0.0).then_inc(preset, 1)
            pool.wait_ge(preset, 1)
            pool.memset(lif[:, 4, :], 0.0).then_inc(preset, 1)
            for i in range(2):
                pool.wait_ge(preset, 2 + 3 * i)
                pool.memset(kst[i][4 * DH:ROWS, :].bitcast(F32), 1.0).then_inc(preset, 1)
                pool.wait_ge(preset, 3 + 3 * i)
                pool.memset(vst[i][:, :, DH:DH + 1], 1.0).then_inc(preset, 1)
                pool.wait_ge(preset, 4 + 3 * i)
                pool.memset(vst[i][:, :, DH + 1:32], 0.0).then_inc(preset, 1)
            pool.sem_inc(tr_done, 2)
            pool.sem_inc(xnt_copied, 2)
            pool.sem_inc(lo_done, QB)
            pool.sem_inc(mx_taken, 2)
            pool.sem_inc(exp_done, 2)
            pool.sem_inc(pv_done, PS)
            for s in range(2):
                pool.sem_inc(stored[s], 32)
                pool.sem_inc(end_out[s], 16)
            pool.sem_inc(squared, 2)
            for free in (v_taken, lif_done):
                pool.sem_inc(free, 1)
            for free in (end_tr, end_trT, end_proj, end_sum):
                pool.sem_inc(free, 2)

            with pool.Fori(0, NB // 2) as n:
                for p in range(2):
                    t = 2 * n + p
                    pool.wait_ge(xb_ready, t + 1)
                    pool.tensor_copy(xnT[:, :, bass.ds(t * BLK, BLK)], xb[:, p]).then_inc(xnt_copied, 1)

            def stage_v(h, b, after):
                pool.wait_ge(pv_done, after)
                pool.tensor_copy(vst[b][:, :, 0:DH],
                                 v_all[:, b * TB:(b + 1) * TB, bass.ds(h * DH, DH)]).then_inc(vst_ready, 1)

            pool.wait_ge(v_taken, NB + 1)
            stage_v(0, 0, PS)

            mem, decayed, upd, acc, zeros, *spks = (lif[:, k, :] for k in range(7))
            LIF_LINKS = 4 * (SPIKES - 1) + 2

            def head(h, b, last=False):
                i = 2 * h + b
                if not last:
                    stage_v(h + b, 1 - b, STEPS * i + PS)
                for part, k in enumerate((UP_A, UP_B)):
                    c = slice(part * FC // 2, (part + 1) * FC // 2)
                    pool.wait_ge(misc_taken, use(i, k) + 1)
                    pool.tensor_tensor(hid_sb[:, c], relu_sb[:, c], relu_sb[:, c], ALU.mult).then_inc(squared, 1)
                n = LIF_LINKS * i
                pool.wait_ge(misc_taken, use(i, DOWN) + 1)
                pool.tensor_tensor(acc, zeros, zeros, ALU.add)
                pool.tensor_scalar(spks[0], y_sb[:], 1.0, None, ALU.is_gt)
                pool.tensor_scalar(decayed, y_sb[:], BETA, None, ALU.mult).then_inc(lif_step, 1)
                for step in range(1, SPIKES):
                    pool.wait_ge(lif_step, n + 1)
                    pool.tensor_tensor(upd, decayed, y_sb[:], ALU.add).then_inc(lif_step, 1)
                    pool.wait_ge(lif_step, n + 2)
                    pool.tensor_tensor(mem, upd, spks[(step + 1) % 2], ALU.subtract).then_inc(lif_step, 1)
                    pool.wait_ge(lif_step, n + 3)
                    pool.tensor_tensor(acc, acc, spks[(step + 1) % 2], ALU.add).then_inc(lif_step, 1)
                    pool.tensor_scalar(spks[step % 2], mem, 1.0, None, ALU.is_gt)
                    pool.tensor_scalar(decayed, mem, BETA, None, ALU.mult).then_inc(lif_step, 1)
                    n += 4
                pool.wait_ge(lif_step, n + 1)
                pool.tensor_tensor(acc, acc, spks[(SPIKES - 1) % 2], ALU.add).then_inc(lif_step, 1)
                pool.wait_ge(lif_step, n + 2)
                pool.tensor_tensor(carrier[:, 1:2], zeros[:, 0:1], zeros[:, 0:1], ALU.add)
                pool.tensor_copy(counts[:, bass.ds(i, 1), :].rearrange("p a d -> p (a d)"), acc).then_inc(lif_done, 1)

            with pool.Fori(0, H - 1) as h:
                for b in range(B):
                    head(h, b)
            head(H - 1, 0)
            head(H - 1, 1, last=True)

            pool.wait_ge(late_in, 64)
            with pool.Fori(0, NB // 2) as n:
                for p in range(2):
                    pool.wait_ge(end_x[p], 16 * (n + 1))
                    pool.tensor_tensor(x_end[p], x_end[p],
                                       bout_sb[:, :].rearrange("p (k d) -> p k d", k=1).broadcast_to([P, KT, D]),
                                       ALU.add).then_inc(end_bias, 1)

        @block.scalar
        def _(act):
            act.wait_ge(const_in, 80)
            act.activation(filt[:, 1, :], filt[:, 0, :], ACT.Exp, scale=-1.0).then_inc(filt_act, 1)
            act.wait_ge(fold_done, 1)
            act.activation(wqk_sb, st[:, 0, :].rearrange("p (c e) -> p c e", c=KC), ACT.Copy).then_inc(fold_taken, 1)

            def deviation(t):
                act.wait_ge(var_ready, t + 1)
                act.activation(rstd[:, 1, :], rstd[:, 0, :], ACT.Sqrt).then_inc(std_ready, 1)

            def take_transposed(t, p):
                act.wait_ge(tr_done, t + 1 + 2)
                act.wait_ge(xnt_copied, t + 1)
                act.activation(xb[:, p], st[:, 0, :].rearrange("p (c e) -> p c e", c=KC),
                               ACT.Copy).then_inc(xb_ready, 1)

            def take_products(t, n, p):
                for w in range(QB):
                    s = w % 2
                    act.wait_ge(qk_ready, QB * t + w + 1)
                    act.wait_ge(stored[s], 32 * ((QB // 2) * t + w // 2 + 1))
                    act.activation(hilo[:, s, 0, :].bitcast(F32R), qk_psum(w), ACT.Copy).then_inc(hi_ready, 1)
                act.wait_ge(v_ready, t + 1)
                act.activation(v_all[:, bass.ds(t * KT, KT), :], st[:, 1, :].rearrange("p (k d) -> p k d", k=KT),
                               ACT.Copy).then_inc(v_taken, 1)

            act.wait_ge(preset, 1)
            act.wait_ge(zero_out, 64)
            deviation(0)
            take_transposed(0, 0)
            with act.Fori(0, NB // 2 - 1) as n:
                for p in range(2):
                    t = 2 * n + p
                    deviation(t + 1)
                    take_transposed(t + 1, 1 - p)
                    take_products(t, n, p)
            deviation(NB - 1)
            take_transposed(NB - 1, 1)
            take_products(NB - 2, NB // 2 - 1, 0)
            take_products(NB - 1, NB // 2 - 1, 1)

            def take_shift(u, landed):
                act.wait_ge(misc_full, u + 1)
                act.wait_ge(shift_in, 32 * landed)
                act.activation(shiftT[:, :].bitcast(F32R), misc[0:16, 0:P], ACT.Copy).then_inc(misc_taken, 1)

            def exponentials(g, s):
                act.wait_ge(score_ready, g + 1)
                act.wait_ge(pv_done, g + 1)
                act.activation(probs[:, s % PS, :], st[:, s % 2, :], ACT.Exp, scale=SCALE).then_inc(exp_done, 1)

            def head(h, b, last=False):
                i = 2 * h + b
                for s in range(FIRST, STEPS + FIRST):
                    if s in (10, 16):
                        k, part = (UP_A, 0) if s == 10 else (UP_B, 1)
                        act.wait_ge(misc_full, use(i, k) + 1)
                        act.wait_ge(squared, 2 * i + part + 1)
                        act.activation(relu_sb[:, part * FC // 2:(part + 1) * FC // 2, :],
                                       misc.rearrange("p (f t) -> p f t", f=FC // 2),
                                       ACT.Relu).then_inc(misc_taken, 1)
                    if s == 12:
                        take_shift(use(i, SHIFT_1), 2 * i + 1)
                    if s == 24:
                        act.wait_ge(misc_full, use(i, DOWN) + 1)
                        act.wait_ge(lif_done, i + 1)
                        act.activation(y_sb[:], misc[:, 0:D], ACT.Copy).then_inc(misc_taken, 1)
                    if s == 28 and not last:
                        take_shift(use(i, SHIFT_0), 2 * i + 2)
                    if s < STEPS or not last:
                        exponentials(STEPS * i + s, s)

            take_shift(0, 0)
            act.wait_ge(xnt_copied, NB + 2)
            for s in range(2):
                act.wait_ge(stored[s], 32 * (QB * NB // 2 + 1))
            for s in range(FIRST):
                exponentials(s, s)
            with act.Fori(0, H - 1) as h:
                for b in range(B):
                    head(h, b)
            head(H - 1, 0)
            head(H - 1, 1, last=True)

            with act.Fori(0, NB // 2) as n:
                for p in range(2):
                    t = 2 * n + p
                    act.wait_ge(end_tr, t + 3)
                    act.wait_ge(end_proj, t + 1)
                    act.activation(attnT_end[:, p], st[:, p, :], ACT.Copy).then_inc(end_trT, 1)

        @block.tensor
        def _(pe):
            pe.wait_ge(const_in, 80)
            pe.wait_ge(filt_dve, NF + 2)
            for w in range(QB):
                for c in range(KC):
                    mm = pe.matmul(st[:, 0, c * BLK + w * P:c * BLK + (w + 1) * P],
                                   wqk_raw[:, w, c * P:(c + 1) * P], filter_acc[(NF - 1) % 2], start=True, stop=True)
            mm.then_inc(fold_done, 1)
            pe.wait_ge(fold_taken, 1)

            def transpose_block(t, p):
                pe.wait_ge(ln_done, t + 1)
                pe.wait_ge(xb_ready, t)
                for c in range(KC):
                    for k in range(KT):
                        mm = pe.transpose(st[:, 0, c * BLK + k * P:c * BLK + (k + 1) * P],
                                          x_norm[:, p, k, c * P:(c + 1) * P], ident[:])
                mm.then_inc(tr_done, 1)

            def project_block(t, p):
                pe.wait_ge(xb_ready, t + 1)
                for w in range(QB):
                    pe.wait_ge(lo_done, QB * t + w + 1)
                    for c in range(KC):
                        mm = pe.matmul(qk_psum(w), wqk_sb[:, c, w * P:(w + 1) * P], xb[:, p, c, :],
                                       start=(c == 0), stop=(c == KC - 1))
                    mm.then_inc(qk_ready, 1)
                pe.wait_ge(v_taken, t + 1)
                for k in range(KT):
                    for c in range(KC):
                        mm = pe.matmul(st[:, 1, k * D:(k + 1) * D], xb[:, p, c, k * P:(k + 1) * P], wv_sb[:, c, :],
                                       start=(c == 0), stop=(c == KC - 1))
                mm.then_inc(v_ready, 1)

            transpose_block(0, 0)
            with pe.Fori(0, NB // 2 - 1) as n:
                for p in range(2):
                    t = 2 * n + p
                    transpose_block(t + 1, 1 - p)
                    project_block(t, p)
            transpose_block(NB - 1, 1)
            project_block(NB - 2, 0)
            project_block(NB - 1, 1)

            def max_chunk(n, unit, b, c):
                tile, chunk = unit // 2, 2 * (unit % 2) + c
                pe.wait_ge(mx_taken, n + 1)
                pe.matmul(mx[:, c, :], qst[b][:, tile * P:(tile + 1) * P], kst[b][:, chunk * BLK:(chunk + 1) * BLK],
                          start=True, stop=True).then_inc(mx_ready, 1)

            def transpose_shift(n, u):
                pe.wait_ge(shift_split, n + 1)
                pe.wait_ge(misc_taken, u)
                pe.matmul(misc[0:16, 0:P], shift[:], ident[:], start=True, stop=True).then_inc(misc_full, 1)

            def scores(g, s, b):
                half, kt = s // TB, s % TB
                pe.wait_ge(exp_done, g + 1)
                for c in range(2):
                    q = half * HALF + c * BLK
                    mm = pe.matmul(st[:, s % 2, c * BLK:(c + 1) * BLK], kst[b][:, kt * P:(kt + 1) * P],
                                   qst[b][:, q:q + BLK], start=True, stop=True)
                mm.then_inc(score_ready, 1)

            def times_v(g, s, b):
                half, kt = s // TB, s % TB
                quarters = probs[:, s % PS, :].rearrange("p (t j q) -> p j t q", j=4, q=32)
                pe.wait_ge(exp_done, g + 1 + 2)
                for j in range(4):
                    mm = pe.matmul(po[32 * j:32 * (j + 1), half * D:(half + 1) * D], vst[b][:, kt, :],
                                   quarters[:, j], start=(kt == 0), stop=(kt == TB - 1))
                mm.then_inc(pv_done, 1)

            def slot(h, b, s, last=False, beside=lambda: None):
                i = 2 * h + b
                g = STEPS * i + s
                unit = (s - LEAD) % UNITS
                maxima = s < LEAD or not last
                mb = b if s < LEAD else 1 - b
                if s == LEAD and maxima:
                    pe.wait_ge(stack_in[mb], STACK * (h + 1 + b))
                n = 2 * (g + UNITS - LEAD)
                if s % 2 == 0 and maxima:
                    max_chunk(n, unit, mb, 0)
                if s < STEPS or not last:
                    if s % STEPS == 0:
                        pe.wait_ge(shift_in, 32 * (2 * i + (3 if s else 1)))
                    if s == TB:
                        pe.wait_ge(shift_in, 32 * (2 * i + 2))
                    scores(g, s % STEPS, b if s < STEPS else 1 - b)
                if s % 2 and maxima:
                    max_chunk(n, unit, mb, 0)
                for v in (s - LAG - 1, s - LAG):
                    if s % 2 and s > LAG and (s - LAG < STEPS or not last):
                        if v % TB == 0:
                            pe.wait_ge(po_taken, 2 * i + v // TB)
                            pe.wait_ge(vst_ready, i + 1 + v // STEPS)
                        times_v(STEPS * i + v, v % STEPS, b if v < STEPS else 1 - b)
                    if maxima and v == s - LAG - 1:
                        max_chunk(n + 1, unit, mb, 1)
                beside()

            def up(f0, tok, last_of):
                for f in (f0, f0 + 1):
                    for c in range(KC):
                        mm = pe.matmul(misc[:, (f % 4) * P:(f % 4 + 1) * P], wfc_sb[:, c, f * P:(f + 1) * P],
                                       xnT[:, c, bass.ds(tok, P)], start=(c == 0), stop=(c == KC - 1))
                if last_of:
                    mm.then_inc(misc_full, 1)

            def down(f0, last_of):
                for f in (f0, f0 + 1):
                    mm = pe.matmul(misc[:, 0:D], hid_sb[:, f, :], wproj_sb[:, f, :],
                                   start=(f == 0), stop=(f == FC - 1))
                if last_of:
                    mm.then_inc(misc_full, 1)

            def head(h, b, last=False):
                i = 2 * h + b

                def beside(s):
                    if s in (6, 8):
                        if s == 6:
                            pe.wait_ge(misc_taken, use(i, UP_A))
                        up(s - 6, i * P, s == 8)
                    if s == 10:
                        transpose_shift(2 * i + 1, use(i, SHIFT_1))
                    if s in (12, 14):
                        if s == 12:
                            pe.wait_ge(misc_taken, use(i, UP_B))
                        up(s - 8, i * P, s == 14)
                    if s in (16, 18, 20, 22):
                        if s == 16:
                            pe.wait_ge(misc_taken, use(i, DOWN))
                        pe.wait_ge(squared, 2 * i + 2 + (1 if s < 20 else 2))
                        down(s - 16, s == 22)
                    if s == 26 and not last:
                        transpose_shift(2 * i + 2, use(i, SHIFT_0))

                for s in range(FIRST, STEPS + FIRST):
                    slot(h, b, s, last, lambda: beside(s))

            pe.wait_ge(stack_in[0], STACK)
            pe.wait_ge(preset, 8)
            pe.wait_ge(lo_done, QB * NB + QB)
            pe.wait_ge(v_taken, NB + 1)
            pe.wait_ge(late_in, 64)
            pe.wait_ge(xnt_copied, NB + 2)
            for unit in range(TB):
                for c in range(2):
                    max_chunk(2 * unit + c, unit, 0, c)
            for unit in range(TB, UNITS - LEAD):
                for c in range(2):
                    max_chunk(2 * unit + c, unit, 0, c)
                if unit == TB + 2:
                    pe.wait_ge(shift_split, 1)
                    pe.matmul(misc[0:16, 0:P], shift[:], ident[:], start=True, stop=True).then_inc(misc_full, 1)
            for s in range(FIRST):
                slot(0, 0, s)
            with pe.Fori(0, H - 1) as h:
                for b in range(B):
                    head(h, b)
            head(H - 1, 0)
            head(H - 1, 1, last=True)

            def end_transpose(t, p):
                pe.wait_ge(end_staged, t + 1)
                pe.wait_ge(end_trT, t + 1)
                for c in range(KC):
                    for k in range(KT):
                        mm = pe.transpose(st[:, p, c * BLK + k * P:c * BLK + (k + 1) * P],
                                          attn_end[:, p, k, c * P:(c + 1) * P], ident[:])
                mm.then_inc(end_tr, 1)

            def end_project(t, p):
                pe.wait_ge(end_trT, t + 3)
                pe.wait_ge(end_sum, t + 1)
                for k in range(KT):
                    for c in range(KC):
                        mm = pe.matmul(proj_end[:, p, k, :],
                                       attnT_end[:, p, c * BLK + k * P:c * BLK + (k + 1) * P], wout_sb[:, c, :],
                                       start=(c == 0), stop=(c == KC - 1))
                mm.then_inc(end_proj, 1)

            end_transpose(0, 0)
            with pe.Fori(0, NB // 2 - 1) as n:
                for p in range(2):
                    t = 2 * n + p
                    end_transpose(t + 1, 1 - p)
                    end_project(t, p)
            end_transpose(NB - 1, 1)
            end_project(NB - 2, 0)
            end_project(NB - 1, 1)

        @block.vector
        def _(dve):
            dve.wait_ge(filt_act, 1)
            dve.tensor_scalar(filt[:, 2, :], filt[:, 1, :], 1.0, None, ALU.add).then_inc(filt_dve, 1)
            dve.wait_ge(filt_dve, 1)
            dve.reciprocal(filt[:, 0, :], filt[:, 2, :]).then_inc(filt_dve, 1)
            dve.wait_ge(filt_dve, 2)
            for f in range(NF):
                to, gate = filter_acc[f % 2], filt[:, 0, f:f + 1]
                if f == 0:
                    dve.tensor_scalar(to, basis_sb[:, f, :], gate, None, ALU.mult).then_inc(filt_dve, 1)
                else:
                    dve.wait_ge(filt_dve, f + 2)
                    dve.scalar_tensor_tensor(out=to, in0=basis_sb[:, f, :], scalar=gate, in1=filter_acc[1 - f % 2],
                                             op0=ALU.mult, op1=ALU.add).then_inc(filt_dve, 1)

            LN_LINKS = 7

            def normalise(t, n, p):
                base = LN_LINKS * t
                dve.wait_ge(x_landed[p], 16 * (n + 1))
                for k in range(KT):
                    last = dve.bn_stats(stats[:, k, :], x_in[:, p, k, :])
                last.then_inc(ln_step, 1)
                dve.wait_ge(ln_step, base + 1)
                dve.memset(carrier[:, 0:1], 0.0)
                for k in range(KT):
                    last = dve.bn_aggr(meanvar[:, k, :], stats[:, k, :])
                last.then_inc(ln_step, 1)
                dve.wait_ge(ln_step, base + 2)
                dve.tensor_scalar(rstd[:, 0, :], meanvar[:, :, 1], EPS, None, ALU.add).then_inc(var_ready, 1)
                dve.wait_ge(std_ready, t + 1)
                dve.reciprocal(rstd[:, 2, :], rstd[:, 1, :]).then_inc(ln_step, 1)
                dve.wait_ge(ln_step, base + 3)
                dve.tensor_tensor(rstd[:, 3, :], rstd[:, 2, :], rstd[:, 2, :], ALU.mult).then_inc(ln_step, 1)
                dve.wait_ge(ln_step, base + 4)
                dve.tensor_tensor(rstd[:, 4, :], rstd[:, 3, :], rstd[:, 0, :], ALU.mult).then_inc(ln_step, 1)
                dve.wait_ge(ln_step, base + 5)
                dve.tensor_scalar(rstd[:, 3, :], rstd[:, 4, :], -0.5, 1.5, ALU.mult, ALU.add).then_inc(ln_step, 1)
                dve.wait_ge(ln_step, base + 6)
                dve.tensor_tensor(rstd[:, 4, :], rstd[:, 3, :], rstd[:, 2, :], ALU.mult).then_inc(ln_step, 1)
                dve.wait_ge(ln_step, base + 7)
                dve.wait_ge(tr_done, t + 1)
                for k in range(KT):
                    last = dve.tensor_scalar(x_norm[:, p, k, :], x_in[:, p, k, :], meanvar[:, k, 0:1],
                                             rstd[:, 4, k:k + 1], ALU.subtract, ALU.mult)
                last.then_inc(ln_done, 1)

            def low_parts(t):
                for w in range(QB):
                    s = w % 2
                    dve.wait_ge(hi_ready, QB * t + w + 1)
                    dve.tensor_tensor(hilo[:, s, 1, :].bitcast(F32R), qk_psum(w), hilo[:, s, 0, :],
                                      ALU.subtract).then_inc(lo_done, 1)

            normalise(0, 0, 0)
            with dve.Fori(0, NB // 2 - 1) as n:
                for p in range(2):
                    t = 2 * n + p
                    normalise(t + 1, n + p, 1 - p)
                    low_parts(t)
            normalise(NB - 1, NB // 2 - 1, 1)
            low_parts(NB - 2)
            low_parts(NB - 1)

            def max_chunk(n, unit, c):
                dve.wait_ge(mx_ready, n + 1)
                tile, chunk = unit // 2, 2 * (unit % 2) + c
                dve.tensor_reduce(pmax[:, tile, chunk:chunk + 1], mx[:, c, :], AX, ALU.max).then_inc(mx_taken, 1)

            def split_shift(n, half, chunks):
                dve.wait_ge(mx_taken, chunks + 2)
                dve.tensor_reduce(nmax[:], pmax[:, half * 8:half * 8 + 8, :], AX, ALU.max, negate=True).then_inc(max_step, 1)
                dve.wait_ge(max_step, 2 * n + 1)
                dve.tensor_copy(shift[:, 0:8].bitcast(F32R), nmax[:]).then_inc(max_step, 1)
                dve.wait_ge(max_step, 2 * n + 2)
                dve.tensor_tensor(shift[:, 8:16].bitcast(F32R), nmax[:], shift[:, 0:8],
                                  ALU.subtract).then_inc(shift_split, 1)

            def normalise_output(h, b, half):
                n = 2 * (2 * h + b) + half
                dve.wait_ge(pv_done, (n + 1) * TB + PS)
                dve.transpose(o_sb[:, half, :, :].rearrange("p t e -> p (t e)"),
                              po[:, half * D:(half + 1) * D]).then_inc(po_taken, 1)
                dve.wait_ge(po_taken, n + 1)
                dve.reciprocal(rden[:], o_sb[:, half, :, DH]).then_inc(den_ready, 1)
                dve.wait_ge(den_ready, n + 1)
                first = b * TB + half * (TB // 2)
                dve.tensor_tensor(attn[:, first:first + TB // 2, bass.ds(h * DH, DH)], o_sb[:, half, :, 0:DH],
                                  rden[:, :].rearrange("p (t a) -> p t a", a=1).broadcast_to([P, TB // 2, DH]),
                                  ALU.mult).then_inc(normalised, 1)

            for unit in range(TB):
                for c in range(2):
                    max_chunk(2 * unit + c, unit, c)
            split_shift(0, 0, 2 * TB)
            for unit in range(TB, UNITS - LEAD):
                for c in range(2):
                    max_chunk(2 * unit + c, unit, c)
            for s in range(FIRST):
                for c in range(2):
                    max_chunk(2 * (s + UNITS - LEAD) + c, (s - LEAD) % UNITS, c)

            def head(h, b, last=False):
                i = 2 * h + b
                for s in range(FIRST, STEPS + FIRST):
                    n = 2 * (STEPS * i + s + UNITS - LEAD)
                    if s < LEAD or not last:
                        for c in range(2):
                            max_chunk(n + c, (s - LEAD) % UNITS, c)
                    if s == LEAD - 1:
                        split_shift(2 * i + 1, 1, n + 2)
                    if s == LEAD + TB - 1 and not last:
                        split_shift(2 * i + 2, 0, n + 2)
                    if s == TB + LAG:
                        normalise_output(h, b, 0)
                    if s == STEPS + LAG:
                        normalise_output(h, b, 1)

            with dve.Fori(0, H - 1) as h:
                for b in range(B):
                    head(h, b)
            head(H - 1, 0)
            head(H - 1, 1, last=True)

            def end_stage(t, p):
                dve.wait_ge(end_tr, t + 1)
                dve.tensor_copy(attn_end[:, p], attn[:, bass.ds(t * KT, KT), :]).then_inc(end_staged, 1)

            def end_base_of(t, n, p):
                dve.wait_ge(end_bias, t + 1)
                dve.wait_ge(end_out[p], 16 * n + 16)
                dve.scalar_tensor_tensor(out=out_end[:, p], in0=counts[:, bass.ds(t * KT, KT), :],
                                         scalar=1.0 / SPIKES, in1=x_end[p],
                                         op0=ALU.mult, op1=ALU.add).then_inc(end_base, 1)

            def end_add(t, p):
                dve.wait_ge(end_base, t + 1)
                dve.wait_ge(end_proj, t + 3)
                dve.tensor_tensor(out_end[:, p], proj_end[:, p], out_end[:, p], ALU.add).then_inc(end_sum, 1)

            dve.wait_ge(normalised, 2 * NT)
            dve.wait_ge(pv_done, STEPS * NT + PS)
            end_stage(0, 0)
            end_stage(1, 1)
            dve.wait_ge(lif_done, NT + 1)
            with dve.Fori(0, NB // 2 - 1) as n:
                for p in range(2):
                    t = 2 * n + p
                    end_base_of(t, n, p)
                    end_stage(t + 2, p)
                    end_add(t, p)
            for t in (NB - 2, NB - 1):
                end_base_of(t, NB // 2 - 1, t % 2)
                end_add(t, t % 2)


def filter_basis():
    e = np.arange(DH)
    one = np.zeros((NF, DH, DH))
    for f in range(NF):
        weight = 1.0 if f in (0, DH // 2) else 2.0
        one[f] = weight / DH * np.cos(2 * np.pi * f * (e[:, None] - e[None, :]) / DH)
    full = np.zeros((P, NF, P), np.float32)
    for g in range(P // DH):
        full[g * DH:(g + 1) * DH, :, g * DH:(g + 1) * DH] = one.transpose(1, 0, 2)
    return full


def kernel(L0_attn_x, L0_attn_w_qkv, L0_attn_w_out, L0_attn_b_out, L0_attn_mask_logits, L0_ffn_W_fc, L0_ffn_W_proj):
    import concourse.bacc as bacc
    from concourse.bass_utils import run_bass_kernel_spmd

    w_qkv = np.asarray(L0_attn_w_qkv)
    wqk = w_qkv[:, 0:2 * D].T.reshape(QB, P, D).transpose(1, 0, 2)
    arrays = {
        "x": np.asarray(L0_attn_x),
        "wqk": wqk,
        "wv": w_qkv[:, 2 * D:3 * D],
        "wout": np.asarray(L0_attn_w_out),
        "bout": np.asarray(L0_attn_b_out),
        "logits": np.asarray(L0_attn_mask_logits),
        "wfc": np.asarray(L0_ffn_W_fc).T,
        "wproj": np.asarray(L0_ffn_W_proj).T,
        "basis": filter_basis(),
        "eye": np.eye(P, dtype=np.float32),
    }
    arrays = {name: np.ascontiguousarray(a) for name, a in arrays.items()}
    nc = bacc.Bacc("TRN2", target_bir_lowering=False, num_devices=1)
    args = {
        name: nc.dram_tensor(name, a.shape, mybir.dt.from_np(a.dtype), kind="ExternalInput").ap()
        for name, a in arrays.items()
    }
    out = nc.dram_tensor("out", (B, S, D), F32, kind="ExternalOutput").ap()
    build(nc, out=out, **args)
    r = run_bass_kernel_spmd(nc, [arrays], core_ids=[0])
    return r.results[0]["out"]
```

```python
from contextlib import ExitStack

import numpy as np

import concourse.bass as bass
from concourse import mybir


P = 128
B, S, D = 2, 2048, 256
H, DH = 16, 16
F = 4 * D
NF = DH // 2 + 1
TOK = B * S
KC = D // P
NT = TOK // P
TB = S // P
BLK = 512
NB = TOK // BLK
KT = BLK // P
QB = 2 * H * DH // P
FC = F // P
HALF = S // 2
ROWS = 4 * DH + 2
UNITS = 2 * TB
STEPS = 2 * TB
LEAD = 8
LAG = 2
FIRST = 6
PS = 4
QK_BANKS = 2
AHEAD = [0, 4, 8, 8]
USES = 5
STACK = 7 * 16
SPIKES = 5
BETA = 0.9
EPS = 1e-5
SCALE = float(DH) ** -0.5

F32 = mybir.dt.float32
F32R = mybir.dt.float32r
BF16 = mybir.dt.bfloat16
ALU = mybir.AluOpType
ACT = mybir.ActivationFunctionType
AX = mybir.AxisListType.X


def build(nc, x, wqk, wv, wout, bout, logits, wfc, wproj, basis, eye, out):
    with ExitStack() as ctx:
        def sb(name, shape, dt=F32):
            return ctx.enter_context(nc.sbuf_tensor(name, shape, dt))

        def sem(name):
            return ctx.enter_context(nc.semaphore(name))

        qk_dram = nc.dram_tensor("qk_scratch", [2, H, 2, DH, TOK], F32, kind="Internal").ap()
        zero_dram = nc.dram_tensor("zero_scratch", [2, S], F32, kind="Internal").ap()

        xnT = sb("xnT", [P, KC, TOK])
        v_all = sb("v_all", [P, NT, D])
        attn = sb("attn", [P, NT, D])
        counts = sb("counts", [P, NT, D], BF16)
        qst = [sb(f"qst{i}", [ROWS, S], F32R) for i in range(2)]
        kst = [sb(f"kst{i}", [ROWS, S], F32R) for i in range(2)]
        probs = sb("probs", [P, PS, HALF])
        vst = [sb(f"vst{i}", [P, TB, 32]) for i in range(2)]
        wfc_sb = sb("wfc_sb", [P, KC, F])
        wproj_sb = sb("wproj_sb", [P, FC, D])
        wout_sb = sb("wout_sb", [P, KC, D])
        bout_sb = sb("bout_sb", [P, D])
        ident = sb("ident", [P, P])
        relu_sb = sb("relu_sb", [P, FC, P])
        hid_sb = sb("hid_sb", [P, FC, P])
        y_sb = sb("y_sb", [P, D])
        lif = sb("lif", [P, 7, D])
        o_sb = sb("o_sb", [P, 2, TB // 2, 32])
        pmax = sb("pmax", [P, TB, 4])
        nmax = sb("nmax", [P, 8])
        shift = sb("shift", [P, 16])
        shiftT = sb("shiftT", [16, P])
        rden = sb("rden", [P, TB // 2])
        stats = sb("stats", [P, KT, 6])
        meanvar = sb("meanvar", [P, KT, 2])
        rstd = sb("rstd", [P, 5, KT])
        carrier = sb("carrier", [P, 2])
        filt = sb("filt", [P, 3, NF])

        x_in = attn[:, 0:2 * KT, :].rearrange("p (b k) d -> p b k d", b=2)
        x_norm = attn[:, 2 * KT:4 * KT, :].rearrange("p (b k) d -> p b k d", b=2)
        xb = probs[:, 0:2, :].rearrange("p b (c t) -> p b c t", c=KC)
        hilo = [t.rearrange("p (c t) -> p c t", c=2) for t in
                (probs[:, 2, :], probs[:, 3, :], relu_sb[:, :, :].rearrange("p f t -> p (f t)"),
                 hid_sb[:, :, :].rearrange("p f t -> p (f t)"))]
        early = counts[:, :, :].bitcast(F32).rearrange("p a b -> p (a b)")
        basis_sb = early[:, 0:NF * P].rearrange("p (f e) -> p f e", f=NF)
        at = NF * P
        wqk_raw = early[:, at:at + QB * D].rearrange("p (b d) -> p b d", b=QB)
        at += QB * D
        wqk_sb = early[:, at:at + KC * QB * P].rearrange("p (c e) -> p c e", c=KC)
        at += KC * QB * P
        wv_sb = early[:, at:at + KC * D].rearrange("p (c e) -> p c e", c=KC)
        at += KC * D
        filter_sb = early[:, at:at + P]
        assert at + 2 * P <= NT * D // 2
        filter_acc = [filter_sb, early[:, at + P:at + 2 * P]]
        x_end = [t[:, :, :].rearrange("p f t -> p (f t)").rearrange("p (k d) -> p k d", k=KT)
                 for t in (relu_sb, hid_sb)]
        attn_end = v_all[:, 0:2 * KT, :].rearrange("p (b k) d -> p b k d", b=2)
        attnT_end = v_all[:, 2 * KT:4 * KT, :].rearrange("p (b k) d -> p b (k d)", b=2)
        out_end = v_all[:, 4 * KT:6 * KT, :].rearrange("p (b k) d -> p b k d", b=2)

        st = ctx.enter_context(nc.psum_tensor("st", [P, 2, HALF], F32))
        banks = ctx.enter_context(nc.psum_tensor("banks", [P, 4, BLK], F32))
        mx, po, misc = banks[:, 0:2, :], banks[:, 2, :], banks[:, 3, :]
        proj_end = banks[:, :, :].rearrange("p (b k) (c d) -> p b (k c) d", b=2, c=2)

        ident_in = sem("ident_in")
        logits_in = sem("logits_in")
        const_in = sem("const_in")
        late_in = sem("late_in")
        preset = sem("preset")
        zero_out = sem("zero_out")
        filt_act = sem("filt_act")
        filt_dve = sem("filt_dve")
        fold_done = sem("fold_done")
        fold_taken = sem("fold_taken")
        x_landed = [sem(f"x_landed{i}") for i in range(2)]
        ln_step = sem("ln_step")
        var_ready = sem("var_ready")
        std_ready = sem("std_ready")
        ln_done = sem("ln_done")
        tr_done = sem("tr_done")
        xb_ready = sem("xb_ready")
        xnt_copied = sem("xnt_copied")
        qk_ready = sem("qk_ready")
        hi_ready = sem("hi_ready")
        lo_done = sem("lo_done")
        stored = [sem(f"stored{i}") for i in range(QB)]
        v_ready = sem("v_ready")
        v_taken = sem("v_taken")
        stack_in = [sem(f"stack_in{i}") for i in range(2)]
        mx_ready = sem("mx_ready")
        mx_taken = sem("mx_taken")
        max_step = sem("max_step")
        shift_split = sem("shift_split")
        shift_in = sem("shift_in")
        score_ready = sem("score_ready")
        exp_done = sem("exp_done")
        pv_done = sem("pv_done")
        vst_ready = sem("vst_ready")
        po_taken = sem("po_taken")
        misc_full = sem("misc_full")
        misc_taken = sem("misc_taken")
        den_ready = sem("den_ready")
        normalised = sem("normalised")
        squared = sem("squared")
        lif_step = sem("lif_step")
        lif_done = sem("lif_done")
        end_x = [sem(f"end_x{i}") for i in range(2)]
        end_staged = sem("end_staged")
        end_spikes = sem("end_spikes")
        end_tr = sem("end_tr")
        end_trT = sem("end_trT")
        end_proj = sem("end_proj")
        end_base = sem("end_base")
        end_sum = sem("end_sum")
        end_out = [sem(f"end_out{i}") for i in range(2)]

        x_blocks = x.rearrange("b (n k p) d -> (b n) p k d", k=KT, p=P)
        out_blocks = out.rearrange("b (n k p) d -> (b n) p k d", k=KT, p=P)

        def use(i, k):
            return USES * i + 1 + k

        UP_A, SHIFT_1, UP_B, DOWN, SHIFT_0 = range(USES)

        def qk_psum(w):
            return banks[:, 2 + w % QK_BANKS, :]

        block = ctx.enter_context(nc.Block())

        @block.sync
        def _(sp):
            def load_x(t, p):
                sp.dma_start(x_in[:, p], x_blocks[t]).then_inc(x_landed[p], 16)

            load_x(0, 0)
            sp.dma_start(filt[:, 0, :], logits.partition_broadcast(P)).then_inc(logits_in, 16)
            sp.dma_start(ident[:], eye).then_inc(ident_in, 16)
            sp.dma_start(basis_sb, basis).then_inc(const_in, 16)
            sp.dma_start(wqk_raw, wqk).then_inc(const_in, 16)
            sp.dma_start(wv_sb, wv.rearrange("(c p) e -> p c e", p=P)).then_inc(const_in, 16)
            load_x(1, 1)
            sp.wait_ge(preset, 1)
            for r in range(2):
                for c in range(2):
                    sp.dma_start(zero_dram[r:r + 1, c * HALF:(c + 1) * HALF],
                                 probs[0:1, 3, :]).then_inc(zero_out, 16)

            def store_block(t):
                for w in range(QB):
                    g = w % 2
                    sp.wait_ge(lo_done, QB * t + w + 1 + QK_BANKS)
                    for part in range(2):
                        dst = qk_dram[w // 2, g * 8:(g + 1) * 8, part, :, bass.ds(t * BLK, BLK)]
                        sp.dma_start(dst, hilo[w][:, part, :]).then_inc(stored[w], 16)

            def load_stack(h, b):
                tok = slice(b * S, (b + 1) * S)
                for part in range(2):
                    for dup in range(2):
                        r = (2 * part + dup) * DH
                        sp.dma_start(qst[b][r:r + DH, :].bitcast(F32), qk_dram[0, h, part, :, tok]).then_inc(stack_in[b], 16)
                sp.dma_start(qst[b][4 * DH:ROWS, :].bitcast(F32), zero_dram).then_inc(stack_in[b], 16)
                for dup in range(2):
                    r = dup * 2 * DH
                    src = qk_dram[1, h, :, :, tok].rearrange("r d t -> (r d) t")
                    sp.dma_start(kst[b][r:r + 2 * DH, :].bitcast(F32), src).then_inc(stack_in[b], 16)

            def store_shift(u, b, half):
                sp.wait_ge(misc_taken, u + 1)
                for r in range(2):
                    dst = qst[b][4 * DH + r:4 * DH + r + 1, half * HALF:(half + 1) * HALF]
                    sp.dma_start(dst.bitcast(F32), shiftT[8 * r:8 * r + 8, :]).then_inc(shift_in, 16)

            def next_x(t, p):
                sp.wait_ge(ln_done, t + 1)
                load_x(t + 2, p)

            with sp.Fori(0, NB // 4) as n:
                for p in range(2):
                    next_x(2 * n + p, p)
                    store_block(2 * n + p)
            for t in range(NB // 2, NB):
                if t < NB - 2:
                    next_x(t, t % 2)
                if t == NB // 2:
                    for w in range(QB):
                        sp.wait_ge(stored[w], 32 * (NB // 2 + 1))
                    sp.wait_ge(zero_out, 64)
                    load_stack(0, 0)
                store_block(t)
                if t == NB // 2:
                    sp.dma_start(wfc_sb[:], wfc.rearrange("(c p) e -> p c e", p=P)).then_inc(late_in, 16)
                if t == NB // 2 + 1:
                    sp.dma_start(wproj_sb[:], wproj.rearrange("(c p) e -> p c e", p=P)).then_inc(late_in, 16)
                if t == NB // 2 + 2:
                    sp.dma_start(wout_sb[:], wout.rearrange("(c p) e -> p c e", p=P)).then_inc(late_in, 16)
                    sp.dma_start(bout_sb[:], bout.partition_broadcast(P)).then_inc(late_in, 16)
            store_shift(0, 0, 0)
            for w in range(QB):
                sp.wait_ge(stored[w], 32 * (NB + 1))

            def head(h, b, last=False):
                i = 2 * h + b
                if not last:
                    sp.wait_ge(exp_done, STEPS * i + 2)
                    load_stack(h + b, 1 - b)
                store_shift(use(i, SHIFT_1), b, 1)
                if not last:
                    store_shift(use(i, SHIFT_0), 1 - b, 0)

            with sp.Fori(0, H - 1) as h:
                for b in range(B):
                    head(h, b)
            head(H - 1, 0)
            head(H - 1, 1, last=True)

            def end_load(t, p):
                sp.dma_start(x_end[p], x_blocks[t]).then_inc(end_x[p], 16)

            sp.wait_ge(misc_full, use(NT - 1, DOWN) + 1)
            end_load(0, 0)
            end_load(1, 1)

            def end_store(t, p):
                sp.wait_ge(end_sum, t + 3)
                sp.dma_start(out_blocks[t], out_end[:, p]).then_inc(end_out[p], 16)

            with sp.Fori(0, NB // 2 - 1) as n:
                for p in range(2):
                    t = 2 * n + p
                    sp.wait_ge(end_spikes, t + 1)
                    end_load(t + 2, p)
                    end_store(t, p)
            for t in range(NB - 2, NB):
                end_store(t, t % 2)
            for p in range(2):
                sp.wait_ge(end_out[p], 16 * (NB // 2 + 1))

        @block.gpsimd
        def _(pool):
            pool.memset(probs[0:1, 3, :], 0.0).then_inc(preset, 1)
            pool.wait_ge(preset, 1)
            pool.memset(lif[:, 4, :], 0.0).then_inc(preset, 1)
            for i in range(2):
                pool.wait_ge(preset, 2 + 3 * i)
                pool.memset(kst[i][4 * DH:ROWS, :].bitcast(F32), 1.0).then_inc(preset, 1)
                pool.wait_ge(preset, 3 + 3 * i)
                pool.memset(vst[i][:, :, DH:DH + 1], 1.0).then_inc(preset, 1)
                pool.wait_ge(preset, 4 + 3 * i)
                pool.memset(vst[i][:, :, DH + 1:32], 0.0).then_inc(preset, 1)
            pool.sem_inc(tr_done, 2)
            pool.sem_inc(xnt_copied, 2)
            pool.sem_inc(lo_done, QK_BANKS)
            pool.sem_inc(mx_taken, 2)
            pool.sem_inc(exp_done, 2)
            pool.sem_inc(pv_done, PS)
            for w in range(QB):
                pool.sem_inc(stored[w], 32)
            for s in range(2):
                pool.sem_inc(end_out[s], 16)
            pool.sem_inc(squared, 2)
            for free in (v_taken, lif_done):
                pool.sem_inc(free, 1)
            for free in (end_tr, end_trT, end_proj, end_sum):
                pool.sem_inc(free, 2)

            with pool.Fori(0, NB // 2) as n:
                for p in range(2):
                    t = 2 * n + p
                    pool.wait_ge(xb_ready, t + 1)
                    pool.tensor_copy(xnT[:, :, bass.ds(t * BLK, BLK)], xb[:, p]).then_inc(xnt_copied, 1)

            def stage_v(h, b, after):
                pool.wait_ge(pv_done, after)
                pool.tensor_copy(vst[b][:, :, 0:DH],
                                 v_all[:, b * TB:(b + 1) * TB, bass.ds(h * DH, DH)]).then_inc(vst_ready, 1)

            pool.wait_ge(v_taken, NB + 1)
            stage_v(0, 0, PS)

            mem, decayed, upd, acc, zeros, *spks = (lif[:, k, :] for k in range(7))
            LIF_LINKS = 4 * (SPIKES - 1) + 2

            def head(h, b, last=False):
                i = 2 * h + b
                if not last:
                    stage_v(h + b, 1 - b, STEPS * i + PS)
                for part, k in enumerate((UP_A, UP_B)):
                    c = slice(part * FC // 2, (part + 1) * FC // 2)
                    pool.wait_ge(misc_taken, use(i, k) + 1)
                    pool.tensor_tensor(hid_sb[:, c], relu_sb[:, c], relu_sb[:, c], ALU.mult).then_inc(squared, 1)
                n = LIF_LINKS * i
                pool.wait_ge(misc_taken, use(i, DOWN) + 1)
                pool.tensor_tensor(acc, zeros, zeros, ALU.add)
                pool.tensor_scalar(spks[0], y_sb[:], 1.0, None, ALU.is_gt)
                pool.tensor_scalar(decayed, y_sb[:], BETA, None, ALU.mult).then_inc(lif_step, 1)
                for step in range(1, SPIKES):
                    pool.wait_ge(lif_step, n + 1)
                    pool.tensor_tensor(upd, decayed, y_sb[:], ALU.add).then_inc(lif_step, 1)
                    pool.wait_ge(lif_step, n + 2)
                    pool.tensor_tensor(mem, upd, spks[(step + 1) % 2], ALU.subtract).then_inc(lif_step, 1)
                    pool.wait_ge(lif_step, n + 3)
                    pool.tensor_tensor(acc, acc, spks[(step + 1) % 2], ALU.add).then_inc(lif_step, 1)
                    pool.tensor_scalar(spks[step % 2], mem, 1.0, None, ALU.is_gt)
                    pool.tensor_scalar(decayed, mem, BETA, None, ALU.mult).then_inc(lif_step, 1)
                    n += 4
                pool.wait_ge(lif_step, n + 1)
                pool.tensor_tensor(acc, acc, spks[(SPIKES - 1) % 2], ALU.add).then_inc(lif_step, 1)
                pool.wait_ge(lif_step, n + 2)
                pool.tensor_tensor(carrier[:, 1:2], zeros[:, 0:1], zeros[:, 0:1], ALU.add)
                pool.tensor_copy(counts[:, bass.ds(i, 1), :].rearrange("p a d -> p (a d)"), acc).then_inc(lif_done, 1)

            with pool.Fori(0, H - 1) as h:
                for b in range(B):
                    head(h, b)
            head(H - 1, 0)
            head(H - 1, 1, last=True)

        @block.scalar
        def _(act):
            act.wait_ge(logits_in, 16)
            act.activation(filt[:, 1, :], filt[:, 0, :], ACT.Exp, scale=-1.0).then_inc(filt_act, 1)

            def deviation(t):
                act.wait_ge(var_ready, t + 1)
                act.activation(rstd[:, 1, :], rstd[:, 0, :], ACT.Sqrt).then_inc(std_ready, 1)

            def take_transposed(t, p):
                act.wait_ge(tr_done, t + 1 + 2)
                act.wait_ge(xnt_copied, t + 1)
                act.activation(xb[:, p], st[:, 0, :].rearrange("p (c e) -> p c e", c=KC),
                               ACT.Copy).then_inc(xb_ready, 1)

            def take_high(t):
                for w in range(QB):
                    act.wait_ge(qk_ready, QB * t + w + 1)
                    act.wait_ge(stored[w], 32 * (t + 1))
                    act.activation(hilo[w][:, 0, :].bitcast(F32R), qk_psum(w), ACT.Copy).then_inc(hi_ready, 1)

            def take_v(t):
                act.wait_ge(v_ready, t + 1)
                act.activation(v_all[:, bass.ds(t * KT, KT), :], st[:, 1, :].rearrange("p (k d) -> p k d", k=KT),
                               ACT.Copy).then_inc(v_taken, 1)

            def take_shift(u, landed):
                act.wait_ge(misc_full, u + 1)
                act.wait_ge(shift_in, 32 * landed)
                act.activation(shiftT[:, :].bitcast(F32R), misc[0:16, 0:P], ACT.Copy).then_inc(misc_taken, 1)

            deviation(0)
            take_transposed(0, 0)
            act.wait_ge(fold_done, 1)
            act.activation(wqk_sb, st[:, 1, :].rearrange("p (c e) -> p c e", c=KC), ACT.Copy).then_inc(fold_taken, 1)
            deviation(1)
            act.wait_ge(zero_out, 64)
            with act.Fori(0, NB // 4) as n:
                for p in range(2):
                    t = 2 * n + p
                    take_high(t)
                    take_transposed(t + 1, 1 - p)
                    deviation(t + 2)
                    take_v(t)
            for t in range(NB // 2, NB):
                take_high(t)
                if t < NB - 1:
                    take_transposed(t + 1, (t + 1) % 2)
                if t < NB - 2:
                    deviation(t + 2)
                if t == NB - 1:
                    take_shift(0, 0)
                take_v(t)

            def exponentials(g, s):
                act.wait_ge(score_ready, g + 1)
                act.wait_ge(pv_done, g + 1)
                act.activation(probs[:, s % PS, :], st[:, s % 2, :], ACT.Exp, scale=SCALE).then_inc(exp_done, 1)

            def head(h, b, last=False):
                i = 2 * h + b
                for s in range(FIRST, STEPS + FIRST):
                    if s in (10, 16):
                        k, part = (UP_A, 0) if s == 10 else (UP_B, 1)
                        act.wait_ge(misc_full, use(i, k) + 1)
                        act.wait_ge(squared, 2 * i + part + 1)
                        act.activation(relu_sb[:, part * FC // 2:(part + 1) * FC // 2, :],
                                       misc.rearrange("p (f t) -> p f t", f=FC // 2),
                                       ACT.Relu).then_inc(misc_taken, 1)
                    if s == 12:
                        take_shift(use(i, SHIFT_1), 2 * i + 1)
                    if s == 24:
                        act.wait_ge(misc_full, use(i, DOWN) + 1)
                        act.wait_ge(lif_done, i + 1)
                        act.activation(y_sb[:], misc[:, 0:D], ACT.Copy).then_inc(misc_taken, 1)
                    if s == 28 and not last:
                        take_shift(use(i, SHIFT_0), 2 * i + 2)
                    if s < STEPS or not last:
                        exponentials(STEPS * i + s, s)

            act.wait_ge(xnt_copied, NB + 2)
            for w in range(QB):
                act.wait_ge(stored[w], 32 * (NB + 1))
            for s in range(FIRST):
                exponentials(s, s)
            with act.Fori(0, H - 1) as h:
                for b in range(B):
                    head(h, b)
            head(H - 1, 0)
            head(H - 1, 1, last=True)

            with act.Fori(0, NB // 2) as n:
                for p in range(2):
                    t = 2 * n + p
                    act.wait_ge(end_tr, t + 3)
                    act.wait_ge(end_proj, t + 1)
                    act.activation(attnT_end[:, p], st[:, p, :], ACT.Copy).then_inc(end_trT, 1)

        @block.tensor
        def _(pe):
            def transpose_block(t, p):
                pe.wait_ge(ln_done, t + 1)
                for c in range(KC):
                    for k in range(KT):
                        mm = pe.transpose(st[:, 0, c * BLK + k * P:c * BLK + (k + 1) * P],
                                          x_norm[:, p, k, c * P:(c + 1) * P], ident[:])
                mm.then_inc(tr_done, 1)

            def fold_filter():
                pe.wait_ge(const_in, 48)
                pe.wait_ge(filt_dve, NF + 2)
                for w in range(QB):
                    for c in range(KC):
                        mm = pe.matmul(st[:, 1, c * BLK + w * P:c * BLK + (w + 1) * P],
                                       wqk_raw[:, w, c * P:(c + 1) * P], filter_acc[(NF - 1) % 2],
                                       start=True, stop=True)
                mm.then_inc(fold_done, 1)

            def max_chunk(n, unit, b, c):
                tile, chunk = unit // 2, 2 * (unit % 2) + c
                pe.wait_ge(mx_taken, n + 1)
                pe.matmul(mx[:, c, :], qst[b][:, tile * P:(tile + 1) * P], kst[b][:, chunk * BLK:(chunk + 1) * BLK],
                          start=True, stop=True).then_inc(mx_ready, 1)

            def first_max(n):
                max_chunk(n, n // 2, 0, n % 2)

            def project_qk(t, p, n=None):
                pe.wait_ge(xb_ready, t + 1)
                for w in range(QB):
                    pe.wait_ge(lo_done, QB * t + w + 1)
                    for c in range(KC):
                        mm = pe.matmul(qk_psum(w), wqk_sb[:, c, w * P:(w + 1) * P], xb[:, p, c, :],
                                       start=(c == 0), stop=(c == KC - 1))
                        if c == KC - 1:
                            mm.then_inc(qk_ready, 1)
                        if n is not None:
                            first_max(n + 2 * w + c)

            def project_v(t, p, n=None, shift=lambda: None):
                pe.wait_ge(v_taken, t + 1)
                for k in range(KT):
                    for c in range(KC):
                        mm = pe.matmul(st[:, 1, k * D:(k + 1) * D], xb[:, p, c, k * P:(k + 1) * P], wv_sb[:, c, :],
                                       start=(c == 0), stop=(c == KC - 1))
                        if k == KT - 1 and c == KC - 1:
                            mm.then_inc(v_ready, 1)
                        if n is not None:
                            first_max(n + 2 * k + c)
                    if k == KT // 2:
                        shift()

            def next_transpose(t, p):
                pe.wait_ge(xb_ready, t)
                transpose_block(t, p)

            pe.wait_ge(ident_in, 16)
            transpose_block(0, 0)
            fold_filter()
            pe.wait_ge(fold_taken, 1)
            with pe.Fori(0, NB // 4) as n:
                for p in range(2):
                    t = 2 * n + p
                    project_qk(t, p)
                    next_transpose(t + 1, 1 - p)
                    project_v(t, p)

            def first_shift():
                pe.wait_ge(shift_split, 1)
                pe.wait_ge(lo_done, QB * NB + QK_BANKS)
                pe.matmul(misc[0:16, 0:P], shift[:], ident[:], start=True, stop=True).then_inc(misc_full, 1)

            chunk = 0
            for t in range(NB // 2, NB):
                units = AHEAD[t - NB // 2]
                if units and not chunk:
                    pe.wait_ge(stack_in[0], STACK)
                    pe.wait_ge(preset, 8)
                project_qk(t, t % 2, chunk if units else None)
                if t < NB - 1:
                    next_transpose(t + 1, (t + 1) % 2)
                project_v(t, t % 2, chunk + 2 * QB if units > QB else None,
                          first_shift if t == NB - 1 else lambda: None)
                chunk += 2 * units

            def transpose_shift(n, u):
                pe.wait_ge(shift_split, n + 1)
                pe.wait_ge(misc_taken, u)
                pe.matmul(misc[0:16, 0:P], shift[:], ident[:], start=True, stop=True).then_inc(misc_full, 1)

            def scores(g, s, b):
                half, kt = s // TB, s % TB
                pe.wait_ge(exp_done, g + 1)
                for c in range(2):
                    q = half * HALF + c * BLK
                    mm = pe.matmul(st[:, s % 2, c * BLK:(c + 1) * BLK], kst[b][:, kt * P:(kt + 1) * P],
                                   qst[b][:, q:q + BLK], start=True, stop=True)
                mm.then_inc(score_ready, 1)

            def times_v(g, s, b):
                half, kt = s // TB, s % TB
                quarters = probs[:, s % PS, :].rearrange("p (t j q) -> p j t q", j=4, q=32)
                pe.wait_ge(exp_done, g + 1 + 2)
                for j in range(4):
                    mm = pe.matmul(po[32 * j:32 * (j + 1), half * D:(half + 1) * D], vst[b][:, kt, :],
                                   quarters[:, j], start=(kt == 0), stop=(kt == TB - 1))
                mm.then_inc(pv_done, 1)

            def slot(h, b, s, last=False, beside=lambda: None):
                i = 2 * h + b
                g = STEPS * i + s
                unit = (s - LEAD) % UNITS
                maxima = s < LEAD or not last
                mb = b if s < LEAD else 1 - b
                if s == LEAD and maxima:
                    pe.wait_ge(stack_in[mb], STACK * (h + 1 + b))
                n = 2 * (g + UNITS - LEAD)
                if s % 2 == 0 and maxima:
                    max_chunk(n, unit, mb, 0)
                if s < STEPS or not last:
                    if s % STEPS == 0:
                        pe.wait_ge(shift_in, 32 * (2 * i + (3 if s else 1)))
                    if s == TB:
                        pe.wait_ge(shift_in, 32 * (2 * i + 2))
                    scores(g, s % STEPS, b if s < STEPS else 1 - b)
                if s % 2 and maxima:
                    max_chunk(n, unit, mb, 0)
                for v in (s - LAG - 1, s - LAG):
                    if s % 2 and s > LAG and (s - LAG < STEPS or not last):
                        if v % TB == 0:
                            pe.wait_ge(po_taken, 2 * i + v // TB)
                            pe.wait_ge(vst_ready, i + 1 + v // STEPS)
                        times_v(STEPS * i + v, v % STEPS, b if v < STEPS else 1 - b)
                    if maxima and v == s - LAG - 1:
                        max_chunk(n + 1, unit, mb, 1)
                beside()

            def up(f0, tok, last_of):
                for f in (f0, f0 + 1):
                    for c in range(KC):
                        mm = pe.matmul(misc[:, (f % 4) * P:(f % 4 + 1) * P], wfc_sb[:, c, f * P:(f + 1) * P],
                                       xnT[:, c, bass.ds(tok, P)], start=(c == 0), stop=(c == KC - 1))
                if last_of:
                    mm.then_inc(misc_full, 1)

            def down(f0, last_of):
                for f in (f0, f0 + 1):
                    mm = pe.matmul(misc[:, 0:D], hid_sb[:, f, :], wproj_sb[:, f, :],
                                   start=(f == 0), stop=(f == FC - 1))
                if last_of:
                    mm.then_inc(misc_full, 1)

            def head(h, b, last=False):
                i = 2 * h + b

                def beside(s):
                    if s in (6, 8):
                        if s == 6:
                            pe.wait_ge(misc_taken, use(i, UP_A))
                        up(s - 6, i * P, s == 8)
                    if s == 10:
                        transpose_shift(2 * i + 1, use(i, SHIFT_1))
                    if s in (12, 14):
                        if s == 12:
                            pe.wait_ge(misc_taken, use(i, UP_B))
                        up(s - 8, i * P, s == 14)
                    if s in (16, 18, 20, 22):
                        if s == 16:
                            pe.wait_ge(misc_taken, use(i, DOWN))
                        pe.wait_ge(squared, 2 * i + 2 + (1 if s < 20 else 2))
                        down(s - 16, s == 22)
                    if s == 26 and not last:
                        transpose_shift(2 * i + 2, use(i, SHIFT_0))

                for s in range(FIRST, STEPS + FIRST):
                    slot(h, b, s, last, lambda: beside(s))

            for n in range(chunk, 2 * (UNITS - LEAD)):
                first_max(n)
            pe.wait_ge(v_taken, NB + 1)
            pe.wait_ge(late_in, 64)
            pe.wait_ge(xnt_copied, NB + 2)
            for s in range(FIRST):
                slot(0, 0, s)
            with pe.Fori(0, H - 1) as h:
                for b in range(B):
                    head(h, b)
            head(H - 1, 0)
            head(H - 1, 1, last=True)

            def end_transpose(t, p):
                pe.wait_ge(end_staged, t + 1)
                pe.wait_ge(end_trT, t + 1)
                for c in range(KC):
                    for k in range(KT):
                        mm = pe.transpose(st[:, p, c * BLK + k * P:c * BLK + (k + 1) * P],
                                          attn_end[:, p, k, c * P:(c + 1) * P], ident[:])
                mm.then_inc(end_tr, 1)

            def end_project(t, p):
                pe.wait_ge(end_trT, t + 3)
                pe.wait_ge(end_sum, t + 1)
                for k in range(KT):
                    for c in range(KC):
                        mm = pe.matmul(proj_end[:, p, k, :],
                                       attnT_end[:, p, c * BLK + k * P:c * BLK + (k + 1) * P], wout_sb[:, c, :],
                                       start=(c == 0), stop=(c == KC - 1))
                mm.then_inc(end_proj, 1)

            end_transpose(0, 0)
            with pe.Fori(0, NB // 2 - 1) as n:
                for p in range(2):
                    t = 2 * n + p
                    end_transpose(t + 1, 1 - p)
                    end_project(t, p)
            end_transpose(NB - 1, 1)
            end_project(NB - 2, 0)
            end_project(NB - 1, 1)

        @block.vector
        def _(dve):
            LN_LINKS = 7

            def normalise(t, n, p):
                base = LN_LINKS * t
                dve.wait_ge(x_landed[p], 16 * (n + 1))
                for k in range(KT):
                    last = dve.bn_stats(stats[:, k, :], x_in[:, p, k, :])
                last.then_inc(ln_step, 1)
                dve.wait_ge(ln_step, base + 1)
                dve.memset(carrier[:, 0:1], 0.0)
                for k in range(KT):
                    last = dve.bn_aggr(meanvar[:, k, :], stats[:, k, :])
                last.then_inc(ln_step, 1)
                dve.wait_ge(ln_step, base + 2)
                dve.tensor_scalar(rstd[:, 0, :], meanvar[:, :, 1], EPS, None, ALU.add).then_inc(var_ready, 1)
                dve.wait_ge(std_ready, t + 1)
                dve.reciprocal(rstd[:, 2, :], rstd[:, 1, :]).then_inc(ln_step, 1)
                dve.wait_ge(ln_step, base + 3)
                dve.tensor_tensor(rstd[:, 3, :], rstd[:, 2, :], rstd[:, 2, :], ALU.mult).then_inc(ln_step, 1)
                dve.wait_ge(ln_step, base + 4)
                dve.tensor_tensor(rstd[:, 4, :], rstd[:, 3, :], rstd[:, 0, :], ALU.mult).then_inc(ln_step, 1)
                dve.wait_ge(ln_step, base + 5)
                dve.tensor_scalar(rstd[:, 3, :], rstd[:, 4, :], -0.5, 1.5, ALU.mult, ALU.add).then_inc(ln_step, 1)
                dve.wait_ge(ln_step, base + 6)
                dve.tensor_tensor(rstd[:, 4, :], rstd[:, 3, :], rstd[:, 2, :], ALU.mult).then_inc(ln_step, 1)
                dve.wait_ge(ln_step, base + 7)
                dve.wait_ge(tr_done, t + 1)
                for k in range(KT):
                    last = dve.tensor_scalar(x_norm[:, p, k, :], x_in[:, p, k, :], meanvar[:, k, 0:1],
                                             rstd[:, 4, k:k + 1], ALU.subtract, ALU.mult)
                last.then_inc(ln_done, 1)

            def build_filter():
                dve.wait_ge(filt_act, 1)
                dve.tensor_scalar(filt[:, 2, :], filt[:, 1, :], 1.0, None, ALU.add).then_inc(filt_dve, 1)
                dve.wait_ge(filt_dve, 1)
                dve.reciprocal(filt[:, 0, :], filt[:, 2, :]).then_inc(filt_dve, 1)
                dve.wait_ge(filt_dve, 2)
                dve.wait_ge(const_in, 48)
                for f in range(NF):
                    to, gate = filter_acc[f % 2], filt[:, 0, f:f + 1]
                    if f == 0:
                        dve.tensor_scalar(to, basis_sb[:, f, :], gate, None, ALU.mult).then_inc(filt_dve, 1)
                    else:
                        dve.wait_ge(filt_dve, f + 2)
                        dve.scalar_tensor_tensor(out=to, in0=basis_sb[:, f, :], scalar=gate, in1=filter_acc[1 - f % 2],
                                                 op0=ALU.mult, op1=ALU.add).then_inc(filt_dve, 1)

            def max_chunk(n, unit, c):
                dve.wait_ge(mx_ready, n + 1)
                tile, chunk = unit // 2, 2 * (unit % 2) + c
                dve.tensor_reduce(pmax[:, tile, chunk:chunk + 1], mx[:, c, :], AX, ALU.max).then_inc(mx_taken, 1)

            def first_max(n):
                max_chunk(n, n // 2, n % 2)

            def low_parts(t, n=None):
                for w in range(QB):
                    if n is not None:
                        for c in range(2):
                            first_max(n + 2 * w + c)
                    dve.wait_ge(hi_ready, QB * t + w + 1)
                    dve.tensor_tensor(hilo[w][:, 1, :].bitcast(F32R), qk_psum(w), hilo[w][:, 0, :],
                                      ALU.subtract).then_inc(lo_done, 1)

            def split_shift(link, n, half, chunks=None):
                if link == 0:
                    dve.wait_ge(mx_taken, chunks + 2)
                    dve.tensor_reduce(nmax[:], pmax[:, half * 8:half * 8 + 8, :], AX, ALU.max,
                                      negate=True).then_inc(max_step, 1)
                if link == 1:
                    dve.wait_ge(max_step, 2 * n + 1)
                    dve.tensor_copy(shift[:, 0:8].bitcast(F32R), nmax[:]).then_inc(max_step, 1)
                if link == 2:
                    dve.wait_ge(max_step, 2 * n + 2)
                    dve.tensor_tensor(shift[:, 8:16].bitcast(F32R), nmax[:], shift[:, 0:8],
                                      ALU.subtract).then_inc(shift_split, 1)

            normalise(0, 0, 0)
            build_filter()
            normalise(1, 0, 1)
            with dve.Fori(0, NB // 4) as n:
                for p in range(2):
                    t = 2 * n + p
                    low_parts(t)
                    normalise(t + 2, n + 1, p)
            chunk = 0
            for t in range(NB // 2, NB):
                units = AHEAD[t - NB // 2]
                low_parts(t, chunk if units else None)
                if t < NB - 2:
                    normalise(t + 2, t // 2 + 1, t % 2)
                if t == NB - 1:
                    for link in range(3):
                        split_shift(link, 0, 0, 2 * TB)
                if units > QB:
                    for n in range(chunk + 2 * QB, chunk + 2 * units):
                        first_max(n)
                chunk += 2 * units
            for n in range(chunk, 2 * (UNITS - LEAD)):
                first_max(n)

            def take_output(h, b, half):
                n = 2 * (2 * h + b) + half
                dve.wait_ge(pv_done, (n + 1) * TB + PS)
                dve.transpose(o_sb[:, half, :, :].rearrange("p t e -> p (t e)"),
                              po[:, half * D:(half + 1) * D]).then_inc(po_taken, 1)

            def normalise_output(h, b, half):
                n = 2 * (2 * h + b) + half
                dve.wait_ge(po_taken, n + 1)
                dve.reciprocal(rden[:], o_sb[:, half, :, DH]).then_inc(den_ready, 1)
                dve.wait_ge(den_ready, n + 1)
                first = b * TB + half * (TB // 2)
                dve.tensor_tensor(attn[:, first:first + TB // 2, bass.ds(h * DH, DH)], o_sb[:, half, :, 0:DH],
                                  rden[:, :].rearrange("p (t a) -> p t a", a=1).broadcast_to([P, TB // 2, DH]),
                                  ALU.mult).then_inc(normalised, 1)

            for s in range(FIRST):
                for c in range(2):
                    max_chunk(2 * (s + UNITS - LEAD) + c, (s - LEAD) % UNITS, c)

            def head(h, b, last=False):
                i = 2 * h + b
                for s in range(FIRST, STEPS + FIRST):
                    n = 2 * (STEPS * i + s + UNITS - LEAD)
                    if s == TB + LAG:
                        take_output(h, b, 0)
                    if s == STEPS + LAG:
                        take_output(h, b, 1)
                    for c in range(2):
                        if s < LEAD or not last:
                            max_chunk(n + c, (s - LEAD) % UNITS, c)
                        for half, start in ((1, LEAD), (0, LEAD + TB)):
                            if 0 <= 2 * (s - start) + c < 3 and (half or not last):
                                split_shift(2 * (s - start) + c, 2 * i + 2 - half, half, n)
                    if s == TB + LAG:
                        normalise_output(h, b, 0)
                    if s == STEPS + LAG:
                        normalise_output(h, b, 1)

            with dve.Fori(0, H - 1) as h:
                for b in range(B):
                    head(h, b)
            head(H - 1, 0)
            head(H - 1, 1, last=True)

            def end_stage(t, p):
                dve.wait_ge(end_tr, t + 1)
                dve.tensor_copy(attn_end[:, p], attn[:, bass.ds(t * KT, KT), :]).then_inc(end_staged, 1)

            def end_base_of(t, n, p):
                dve.wait_ge(end_x[p], 16 * (n + 1))
                dve.wait_ge(end_out[p], 16 * n + 16)
                dve.scalar_tensor_tensor(out=out_end[:, p], in0=counts[:, bass.ds(t * KT, KT), :],
                                         scalar=1.0 / SPIKES, in1=x_end[p],
                                         op0=ALU.mult, op1=ALU.add).then_inc(end_spikes, 1)
                dve.wait_ge(end_spikes, t + 1)
                dve.tensor_tensor(out_end[:, p], out_end[:, p],
                                  bout_sb[:, :].rearrange("p (k d) -> p k d", k=1).broadcast_to([P, KT, D]),
                                  ALU.add).then_inc(end_base, 1)

            def end_add(t, p):
                dve.wait_ge(end_base, t + 1)
                dve.wait_ge(end_proj, t + 3)
                dve.tensor_tensor(out_end[:, p], proj_end[:, p], out_end[:, p], ALU.add).then_inc(end_sum, 1)

            dve.wait_ge(normalised, 2 * NT)
            dve.wait_ge(pv_done, STEPS * NT + PS)
            end_stage(0, 0)
            end_stage(1, 1)
            dve.wait_ge(late_in, 64)
            dve.wait_ge(lif_done, NT)
            with dve.Fori(0, NB // 2 - 1) as n:
                for p in range(2):
                    t = 2 * n + p
                    end_base_of(t, n, p)
                    end_stage(t + 2, p)
                    end_add(t, p)
            end_base_of(NB - 2, NB // 2 - 1, 0)
            end_add(NB - 2, 0)
            dve.wait_ge(lif_done, NT + 1)
            end_base_of(NB - 1, NB // 2 - 1, 1)
            end_add(NB - 1, 1)


def filter_basis():
    e = np.arange(DH)
    one = np.zeros((NF, DH, DH))
    for f in range(NF):
        weight = 1.0 if f in (0, DH // 2) else 2.0
        one[f] = weight / DH * np.cos(2 * np.pi * f * (e[:, None] - e[None, :]) / DH)
    full = np.zeros((P, NF, P), np.float32)
    for g in range(P // DH):
        full[g * DH:(g + 1) * DH, :, g * DH:(g + 1) * DH] = one.transpose(1, 0, 2)
    return full


def kernel(L0_attn_x, L0_attn_w_qkv, L0_attn_w_out, L0_attn_b_out, L0_attn_mask_logits, L0_ffn_W_fc, L0_ffn_W_proj):
    import concourse.bacc as bacc
    from concourse.bass_utils import run_bass_kernel_spmd

    w_qkv = np.asarray(L0_attn_w_qkv)
    wqk = w_qkv[:, 0:2 * D].T.reshape(QB, P, D).transpose(1, 0, 2)
    arrays = {
        "x": np.asarray(L0_attn_x),
        "wqk": wqk,
        "wv": w_qkv[:, 2 * D:3 * D],
        "wout": np.asarray(L0_attn_w_out),
        "bout": np.asarray(L0_attn_b_out),
        "logits": np.asarray(L0_attn_mask_logits),
        "wfc": np.asarray(L0_ffn_W_fc).T,
        "wproj": np.asarray(L0_ffn_W_proj).T,
        "basis": filter_basis(),
        "eye": np.eye(P, dtype=np.float32),
    }
    arrays = {name: np.ascontiguousarray(a) for name, a in arrays.items()}
    nc = bacc.Bacc("TRN2", target_bir_lowering=False, num_devices=1)
    args = {
        name: nc.dram_tensor(name, a.shape, mybir.dt.from_np(a.dtype), kind="ExternalInput").ap()
        for name, a in arrays.items()
    }
    out = nc.dram_tensor("out", (B, S, D), F32, kind="ExternalOutput").ap()
    build(nc, out=out, **args)
    r = run_bass_kernel_spmd(nc, [arrays], core_ids=[0])
    return r.results[0]["out"]
```
